# Optimizing a Trainium2 kernel written in Bass

```python
import numpy as np
import jax
import jax.numpy as jnp

def _softmax(x, axis=-1):
    return jax.nn.softmax(x, axis=axis)

def _gelu(x):
    return jax.nn.gelu(x, approximate=True)

def _silu(x):
    return jax.nn.silu(x)

def _sigmoid(x):
    return jax.nn.sigmoid(x)

def _layernorm(x, axis=-1, eps=1e-05):
    m = jnp.mean(x, axis=axis, keepdims=True)
    v = jnp.var(x, axis=axis, keepdims=True)
    return (x - m) / jnp.sqrt(v + eps)

def _scatter_add(tgt, idx, src, axis=0):
    return tgt.at[idx].add(src)

def _segment_sum(src, seg, n):
    return jax.ops.segment_sum(src, seg, n)
kernel_name = 'mk_hybrid_d1_jaxref_r8_fdc454'

def setup_inputs(seed: int=0):
    np.random.seed(seed)
    _w = jnp.asarray

    def _L0_attn_a_setup():
        import jax, jax.numpy as jnp
        import numpy as np
        N_HEADS = 32
        N_KV_HEADS = 8
        DIM = 512
        HEAD_DIM = DIM // N_HEADS
        N_REP = N_HEADS // N_KV_HEADS
        ROPE_THETA = 10000.0

        def _apply_rope(x):
            seq = x.shape[2]
            hd = x.shape[-1]
            inv_freq = 1.0 / ROPE_THETA ** (jnp.arange(0, hd, 2, dtype=jnp.float32) / hd)
            angles = jnp.arange(seq, dtype=jnp.float32)[:, None] * inv_freq[None, :]
            cos = jnp.cos(angles)[None, None]
            sin = jnp.sin(angles)[None, None]
            x1 = x[..., 0::2]
            x2 = x[..., 1::2]
            r1 = x1 * cos - x2 * sin
            r2 = x1 * sin + x2 * cos
            return jnp.stack([r1, r2], axis=-1).reshape(x.shape)
        key = jax.random.key(seed)
        k1, k2, k3 = jax.random.split(key, 3)
        bs, seq = (1, 256)
        x = jax.random.normal(k1, (bs, seq, DIM), dtype=jnp.float32)
        w_qkv = jax.random.normal(k2, (DIM, HEAD_DIM * (N_HEADS + 2 * N_KV_HEADS)), dtype=jnp.float32) * 0.02
        w_o = jax.random.normal(k3, (N_HEADS * HEAD_DIM, DIM), dtype=jnp.float32) * 0.02
        return {'x': x, 'w_qkv': w_qkv, 'w_o': w_o}
    _L0_attn_a_in = _L0_attn_a_setup()

    def _L0_attn_b_setup():
        import jax, jax.numpy as jnp
        import numpy as np
        DIM = 512
        N_HEADS = 32
        N_KV_HEADS = 8
        HEAD_DIM = DIM // N_HEADS
        N_REP = N_HEADS // N_KV_HEADS
        ROPE_BASE = 500000.0
        B, S = (2, 256)

        def _rope_cos_sin(seq_len, head_dim):
            inv_freq = 1.0 / ROPE_BASE ** (jnp.arange(0, head_dim, 2, dtype=jnp.float32) / head_dim)
            t = jnp.arange(seq_len, dtype=jnp.float32)
            freqs = jnp.outer(t, inv_freq)
            return (jnp.cos(freqs), jnp.sin(freqs))

        def _apply_rope(x, cos, sin):
            half = x.shape[-1] // 2
            x1, x2 = (x[..., :half], x[..., half:])
            return jnp.concatenate([x1 * cos - x2 * sin, x2 * cos + x1 * sin], axis=-1)
        key = jax.random.key(seed)
        k1, k2, k3 = jax.random.split(key, 3)
        x = jax.random.normal(k1, (B, S, DIM), dtype=jnp.float32)
        qkv_out = (N_HEADS + 2 * N_KV_HEADS) * HEAD_DIM
        w_qkv = jax.random.normal(k2, (qkv_out, DIM), dtype=jnp.float32) * DIM ** (-0.5)
        w_o = jax.random.normal(k3, (DIM, DIM), dtype=jnp.float32) * DIM ** (-0.5)
        return {'x': x, 'w_qkv': w_qkv, 'w_o': w_o}
    _L0_attn_b_in = _L0_attn_b_setup()

    def _L0_ffn_setup():
        import jax, jax.numpy as jnp
        import numpy as np
        import math
        IN_DIM = 512
        FEATURES = 512
        BATCH, SEQ = (8, 256)
        key = jax.random.key(seed)
        kx, kk = jax.random.split(key)
        x = jax.random.normal(kx, (BATCH, SEQ, IN_DIM), dtype=jnp.float32)
        kernel = jax.random.randint(kk, (IN_DIM, FEATURES), 0, 2) > 0
        scale = jnp.asarray(1.0 / math.sqrt(IN_DIM), dtype=jnp.float32)
        return {'x': x, 'kernel': kernel, 'scale': scale}
    _L0_ffn_in = _L0_ffn_setup()
    _d = {'L0_attn_a_x': _L0_attn_a_in['x'], 'L0_attn_a_w_qkv': _L0_attn_a_in['w_qkv'], 'L0_attn_a_w_o': _L0_attn_a_in['w_o'], 'L0_attn_b_w_qkv': _L0_attn_b_in['w_qkv'], 'L0_attn_b_w_o': _L0_attn_b_in['w_o'], 'L0_ffn_kernel': _L0_ffn_in['kernel'], 'L0_ffn_scale': _L0_ffn_in['scale']}
    _x0 = _d['L0_attn_a_x']
    _d['L0_attn_a_x'] = jax.random.normal(jax.random.fold_in(jax.random.key(seed), 1), (2, 1024, 512), dtype=_x0.dtype)
    del _x0
    return _d

def reference(L0_attn_a_x, L0_attn_a_w_qkv, L0_attn_a_w_o, L0_attn_b_w_qkv, L0_attn_b_w_o, L0_ffn_kernel, L0_ffn_scale):

    def _L0_attn_a_ref(x, w_qkv, w_o):
        import jax, jax.numpy as jnp
        import numpy as np
        N_HEADS = 32
        N_KV_HEADS = 8
        DIM = 512
        HEAD_DIM = DIM // N_HEADS
        N_REP = N_HEADS // N_KV_HEADS
        ROPE_THETA = 10000.0

        def _apply_rope(x):
            seq = x.shape[2]
            hd = x.shape[-1]
            inv_freq = 1.0 / ROPE_THETA ** (jnp.arange(0, hd, 2, dtype=jnp.float32) / hd)
            angles = jnp.arange(seq, dtype=jnp.float32)[:, None] * inv_freq[None, :]
            cos = jnp.cos(angles)[None, None]
            sin = jnp.sin(angles)[None, None]
            x1 = x[..., 0::2]
            x2 = x[..., 1::2]
            r1 = x1 * cos - x2 * sin
            r2 = x1 * sin + x2 * cos
            return jnp.stack([r1, r2], axis=-1).reshape(x.shape)
        bs, seq, _ = x.shape
        qkv = x @ w_qkv
        q_sz = N_HEADS * HEAD_DIM
        kv_sz = N_KV_HEADS * HEAD_DIM
        xq = qkv[..., :q_sz].reshape(bs, seq, N_HEADS, HEAD_DIM).transpose(0, 2, 1, 3)
        xk = qkv[..., q_sz:q_sz + kv_sz].reshape(bs, seq, N_KV_HEADS, HEAD_DIM).transpose(0, 2, 1, 3)
        xv = qkv[..., q_sz + kv_sz:].reshape(bs, seq, N_KV_HEADS, HEAD_DIM).transpose(0, 2, 1, 3)
        xq = _apply_rope(xq)
        xk = _apply_rope(xk)
        keys = jnp.repeat(xk, N_REP, axis=1)
        values = jnp.repeat(xv, N_REP, axis=1)
        scale = 1.0 / jnp.sqrt(jnp.float32(HEAD_DIM))
        scores = jnp.einsum('bhsd,bhtd->bhst', xq, keys) * scale
        causal = jnp.tril(jnp.ones((seq, seq), dtype=bool))[None, None]
        scores = jnp.where(causal, scores, -jnp.inf)
        probs = jax.nn.softmax(scores, axis=-1)
        out = jnp.einsum('bhst,bhtd->bhsd', probs, values)
        out = out.transpose(0, 2, 1, 3).reshape(bs, seq, N_HEADS * HEAD_DIM)
        return out @ w_o

    def _L0_attn_b_ref(x, w_qkv, w_o):
        import jax, jax.numpy as jnp
        import numpy as np
        DIM = 512
        N_HEADS = 32
        N_KV_HEADS = 8
        HEAD_DIM = DIM // N_HEADS
        N_REP = N_HEADS // N_KV_HEADS
        ROPE_BASE = 500000.0
        B, S = (2, 256)

        def _rope_cos_sin(seq_len, head_dim):
            inv_freq = 1.0 / ROPE_BASE ** (jnp.arange(0, head_dim, 2, dtype=jnp.float32) / head_dim)
            t = jnp.arange(seq_len, dtype=jnp.float32)
            freqs = jnp.outer(t, inv_freq)
            return (jnp.cos(freqs), jnp.sin(freqs))

        def _apply_rope(x, cos, sin):
            half = x.shape[-1] // 2
            x1, x2 = (x[..., :half], x[..., half:])
            return jnp.concatenate([x1 * cos - x2 * sin, x2 * cos + x1 * sin], axis=-1)
        batch, seq_len, _ = x.shape
        qkv = jnp.einsum('bsd,od->bso', x, w_qkv)
        q_size = N_HEADS * HEAD_DIM
        kv_size = N_KV_HEADS * HEAD_DIM
        q = qkv[:, :, :q_size].reshape(batch, seq_len, N_HEADS, HEAD_DIM).transpose(0, 2, 1, 3)
        k = qkv[:, :, q_size:q_size + kv_size].reshape(batch, seq_len, N_KV_HEADS, HEAD_DIM).transpose(0, 2, 1, 3)
        v = qkv[:, :, q_size + kv_size:].reshape(batch, seq_len, N_KV_HEADS, HEAD_DIM).transpose(0, 2, 1, 3)
        cos, sin = _rope_cos_sin(seq_len, HEAD_DIM)
        cos = cos[None, None]
        sin = sin[None, None]
        q = _apply_rope(q, cos, sin)
        k = _apply_rope(k, cos, sin)
        k = jnp.repeat(k, N_REP, axis=1)
        v = jnp.repeat(v, N_REP, axis=1)
        scale = 1.0 / np.sqrt(HEAD_DIM).astype(np.float32)
        scores = jnp.einsum('bhqd,bhkd->bhqk', q, k) * scale
        causal = jnp.tril(jnp.ones((seq_len, seq_len), dtype=bool))
        scores = jnp.where(causal, scores, jnp.finfo(scores.dtype).min)
        attn = jax.nn.softmax(scores, axis=-1)
        out = jnp.einsum('bhqk,bhkd->bhqd', attn, v)
        out = out.transpose(0, 2, 1, 3).reshape(batch, seq_len, N_HEADS * HEAD_DIM)
        return jnp.einsum('bso,do->bsd', out, w_o)

    def _L0_ffn_ref(x, kernel, scale):
        import jax, jax.numpy as jnp
        import numpy as np
        import math
        IN_DIM = 512
        FEATURES = 512
        BATCH, SEQ = (8, 256)
        w = kernel.astype(x.dtype) * 2.0 - 1.0
        return scale * jnp.einsum('bsi,if->bsf', x, w)
    x = L0_attn_a_x
    x = x + _L0_attn_a_ref(_layernorm(x, axis=-1), L0_attn_a_w_qkv, L0_attn_a_w_o)
    x = x + _L0_ffn_ref(_layernorm(x, axis=-1), L0_ffn_kernel, L0_ffn_scale)
    x = x + _L0_attn_b_ref(_layernorm(x, axis=-1), L0_attn_b_w_qkv, L0_attn_b_w_o)
    x = x + _L0_ffn_ref(_layernorm(x, axis=-1), L0_ffn_kernel, L0_ffn_scale)
    return x

_drawn_inputs = setup_inputs


def setup_inputs(seed=0):
    import zlib

    import numpy as np

    out = dict(_drawn_inputs(seed))
    spreads = {}
    factors = {}
    for name, (base, spread) in spreads.items():
        noise = np.random.default_rng([zlib.crc32(name.encode()), seed]).standard_normal(out[name].shape)
        drawn = base * np.exp(spread * noise) if base else spread * noise
        out[name] = jnp.asarray(drawn.astype(out[name].dtype))
    for name, factor in factors.items():
        out[name] = (out[name] * factor).astype(out[name].dtype)
    return out
```

```python
from contextlib import ExitStack

import concourse.bass as bass
from concourse import mybir

ALU = mybir.AluOpType
ACT = mybir.ActivationFunctionType
AX = mybir.AxisListType
F32 = mybir.dt.float32
BF16 = mybir.dt.bfloat16
U8 = mybir.dt.uint8

P = 128
SEQ = 1024
DIM = 512
HEADS = 32
KV = 8
REP = HEADS // KV
HD = DIM // HEADS
HALF = HD // 2
BATCH = 2
LAYERS = 2
EPS = 1e-5

TILES = SEQ // P
PAIRS = TILES // 2
KC = DIM // P
QKV = DIM + 2 * KV * HD
QK = DIM + KV * HD
QCHUNK = 512
CHUNKS = SEQ // QCHUNK
QT_PER_CHUNK = QCHUNK // P
VW = 32
PSLOTS = 3

SLOTS = 8
MAXROW = (SLOTS - 1) * HD


class Signal:

    def __init__(self, sem, credit=0):
        self.sem, self.credit = sem, credit

    def after(self, n):
        return n + (self.credit + 1)


def score_steps():
    out = []
    for c in range(CHUNKS):
        for kb in range((c + 1) * QT_PER_CHUNK):
            q0 = max(c * QCHUNK, kb * P)
            out.append((c, kb, q0, (c + 1) * QCHUNK - q0))
    return out


def max_units():
    out = []
    for qt in range(TILES):
        keys = (qt + 1) * P
        per = max(1, 2 * (QCHUNK // keys)) if keys <= QCHUNK else 1
        per = min(per, REP)
        out += [(qt, list(range(h, h + per))) for h in range(0, REP, per)]
    return out


STEPS = score_steps()
UNITS = max_units()
NS = len(STEPS)
NU = len(UNITS)
ND = TILES
UNITS_0 = sum(1 for qt, _ in UNITS if qt < QT_PER_CHUNK)
FIRST_1 = QT_PER_CHUNK
assert NS % PSLOTS == 0 and NU % 2 == 0


def group_order(has_prev, has_next):
    out, unit = [], 0
    for s in range(NS):
        out.append(("S", s))
        if s == 0:
            out.append(("N", 1, 0))
        if s == 1 and has_prev:
            out.append(("O", 1, -1))
        if has_next:
            upto = min(NU, (s + 1) * NU // (NS - 1))
            while unit < upto:
                out.append(("U", unit))
                unit += 1
            if s == 6:
                out.append(("N", 0, 1))
        if s >= 2:
            out.append(("PV", s - 2))
        if s == 7:
            out.append(("O", 0, 0))
    out += [("PV", NS - 2), ("PV", NS - 1)]
    return out


READY = 4
LN_LINKS = 6
NM_LINKS = 4


def build(nc, x, w_qkv, w_o, w_ffn, scale, cos, sin, eye, tri, out):
    with ExitStack() as ctx:
        def sb(name, shape, dt=F32):
            return ctx.enter_context(nc.sbuf_tensor(name, shape, dt))

        def ps(name, shape, dt=F32):
            return ctx.enter_context(nc.psum_tensor(name, shape, dt))

        def sem(name):
            return ctx.enter_context(nc.semaphore(name))

        xs = sb("xs", [P, TILES, DIM])
        wq_s = sb("wq_s", [P, KC, QKV])
        wo_s = sb("wo_s", [P, KC, DIM])
        wf_s = sb("wf_s", [P, KC, DIM])
        cos_s = sb("cos_s", [P, LAYERS, TILES, HD])
        sin_s = sb("sin_s", [P, LAYERS, TILES, HD])
        ident = sb("ident", [P, P])
        ident_b = sb("ident_b", [P, P], BF16)
        tri_b = sb("tri_b", [P, P], BF16)
        scale_s = sb("scale_s", [P, 1])
        eps_s = sb("eps_s", [P, 1])

        stats = sb("stats", [P, 2, 6])
        mv = sb("mv", [P, 2, 2])
        var_eps = sb("var_eps", [P, 2])
        ln_var = sb("ln_var", [P, 2])
        rs0 = sb("rs0", [P, 2])
        newton = sb("newton", [P, 2])
        newton2 = sb("newton2", [P, 2])
        rstd = sb("rstd", [P, 2])
        xn = sb("xn", [P, 2, DIM])
        xc = sb("xc", [P, 2, DIM])
        xnT = sb("xnT", [P, 2, KC, P])
        xcT = sb("xcT", [P, 2, KC, P])

        qT = sb("qT", [P, HEADS, SEQ], BF16)
        kT = sb("kT", [P, KV, SEQ], BF16)
        vs = sb("vs", [P, TILES, KV, VW])
        v_grp = sb("v_grp", [P, TILES, VW])
        k_rec = sb("k_rec", [P, 2, KV, SLOTS, HD], BF16)
        o_T = sb("o_T", [P, CHUNKS, QCHUNK])
        mx = sb("mx", [P, TILES, REP])
        nm = sb("nm", [P, QT_PER_CHUNK, REP])
        nm_r = sb("nm_r", [P, QT_PER_CHUNK, REP])
        nm_parts = sb("nm_parts", [P, CHUNKS, QT_PER_CHUNK, 3, REP], BF16)
        nm_rows = sb("nm_rows", [3 * REP, CHUNKS, QCHUNK], BF16)
        den = sb("den", [P, QT_PER_CHUNK, REP])

        attn = sb("attn", [P, TILES, DIM])
        q_rec = attn[:].rearrange("p t d -> p (t d)").bitcast(BF16).rearrange(
            "p (b h s d) -> p b h s d", b=2, h=HEADS, s=SLOTS)
        probs = sb("probs", [P, PSLOTS, REP, QCHUNK])
        rows = probs[:].rearrange("p a b c -> p (a b c)")
        qk = rows[:, 0:2 * QK].rearrange("p (b n) -> p b n", b=2)
        r_s = rows[:, 2 * QK:4 * QK].rearrange("p (b n) -> p b n", b=2)
        t_s = rows[:, 4 * QK:6 * QK].rearrange("p (b n) -> p b n", b=2)
        wf_raw = sb("wf_raw", [P, KC, DIM], U8)

        psM = ps("psM", [P, 4, 512])
        psE = ps("psE", [P, 2, 512])
        psO = ps("psO", [P, 512])
        psT = ps("psT", [P, 512])
        rec_banks = [psT[:].bitcast(BF16), psO[:].bitcast(BF16)]
        nm_ps = psT[:].bitcast(BF16)

        consts_in = sem("consts_in")
        ready = sem("ready")
        x_in = [sem(f"x_in{i}") for i in range(PAIRS)]
        x_out = sem("x_out")
        wq_in, wo_in = sem("wq_in"), sem("wo_in")
        ln_self = Signal(sem("ln_self"))
        var_ready = Signal(sem("var_ready"))
        ln_done = Signal(sem("ln_done"))
        rs_ready = Signal(sem("rs_ready"))
        xn_ready = Signal(sem("xn_ready"))
        xn_turned = Signal(sem("xn_turned"), 2)
        xnT_ready = Signal(sem("xnT_ready"))
        qkv_ready = Signal(sem("qkv_ready"), 2)
        qk_ready = Signal(sem("qk_ready"))
        qkv_used = Signal(sem("qkv_used"), 2)
        sin_ready = Signal(sem("sin_ready"))
        cos_self = Signal(sem("cos_self"))
        rope_ready = Signal(sem("rope_ready"))
        h_ready = Signal(sem("h_ready"))
        r1_ready = Signal(sem("r1_ready"))
        m_ready = Signal(sem("m_ready"))
        rec_ready = Signal(sem("rec_ready"), 2)
        rec_turned = Signal(sem("rec_turned"), 5 * 2)
        rec_dve = Signal(sem("rec_dve"), 3)
        rec_act = Signal(sem("rec_act"), 2)
        unit_ready = Signal(sem("unit_ready"))
        unit_used = Signal(sem("unit_used"), 2)
        nm_split = Signal(sem("nm_split"), 2)
        nm_self = Signal(sem("nm_self"))
        nm_turned = Signal(sem("nm_turned"), 2)
        nm_copied = Signal(sem("nm_copied"))
        nm_in = [sem(f"nm_in{c}") for c in range(CHUNKS)]
        st_ready = Signal(sem("st_ready"))
        p_ready = Signal(sem("p_ready"), 2)
        masked = Signal(sem("masked"))
        v_ready = Signal(sem("v_ready"))
        pv_done = Signal(sem("pv_done"), NS)
        o_copied = Signal(sem("o_copied"), 2)
        o_turned = Signal(sem("o_turned"), 2)
        o_self = Signal(sem("o_self"))
        o_done = Signal(sem("o_done"), 2)
        xc_ready = Signal(sem("xc_ready"))
        xc_turned = Signal(sem("xc_turned"), 2)
        xcT_ready = Signal(sem("xcT_ready"))
        wo_ready = Signal(sem("wo_ready"), 8)
        wo_added = Signal(sem("wo_added"), 2)
        xd_turned = Signal(sem("xd_turned"), 2)
        xdT_ready = Signal(sem("xdT_ready"))
        ffn_ready = Signal(sem("ffn_ready"), 2)
        ffn_added = Signal(sem("ffn_added"), 8)

        block = ctx.enter_context(nc.Block())

        passed = sem("passed")

        def wait_alone(eng, signal, value):
            eng.wait_ge(signal, value)
            eng.sem_inc(passed, 1)

        def rounds(eng, body):
            with eng.Fori(0, BATCH) as b:
                with eng.Fori(0, LAYERS) as l:
                    body(b, l, b * LAYERS + l)

        @block.sync
        def _(sp):
            wv = w_ffn.rearrange("(c p) n -> p c n", p=P)
            sp.dma_start(ident[:], eye).then_inc(consts_in, 16)
            sp.dma_start(wf_raw[:], wv).then_inc(consts_in, 16)
            sp.dma_start(cos_s[:], cos).then_inc(consts_in, 16)
            sp.dma_start(sin_s[:], sin).then_inc(consts_in, 16)
            sp.dma_start(scale_s[:], scale.rearrange("(a b) -> a b", a=1).to_broadcast([P, 1])).then_inc(consts_in, 16)
            sp.dma_start(rows[:, 0:P], tri).then_inc(consts_in, 16)

            for s in (x_out, *nm_in):
                sp.sem_inc(s, 16)

            with sp.Fori(0, BATCH) as b:
                for i in range(PAIRS):
                    sp.wait_ge(x_out, b * (16 * PAIRS) + 16)
                    src = x[b].rearrange("(t p) d -> p t d", p=P)[:, 2 * i:2 * i + 2, :]
                    sp.dma_start(xs[:, 2 * i:2 * i + 2, :], src).then_inc(x_in[i], 16)
                with sp.Fori(0, LAYERS) as l:
                    r = b * LAYERS + l
                    sp.wait_ge(qkv_ready.sem, r * TILES + qkv_ready.credit)
                    sp.dma_start(wq_s[:], w_qkv[l].rearrange("(c p) n -> p c n", p=P)).then_inc(wq_in, 16)
                    sp.wait_ge(wo_ready.sem, r * TILES + wo_ready.credit)
                    sp.dma_start(wo_s[:], w_o[l].rearrange("(c p) n -> p c n", p=P)).then_inc(wo_in, 16)
                    with sp.Fori(0, KV) as g:
                        for c in range(CHUNKS):
                            sp.wait_ge(nm_copied.sem, nm_copied.after((r * KV + g) * CHUNKS + c))
                            sp.dma_start(
                                qT[MAXROW:MAXROW + 3, bass.ds(g * REP, REP), c * QCHUNK:(c + 1) * QCHUNK],
                                nm_rows[:, c, :],
                            ).then_inc(nm_in[c], 16)
                for i in range(PAIRS):
                    sp.wait_ge(ffn_added.sem, ffn_added.after(b * (LAYERS * TILES) + ((LAYERS - 1) * TILES + 2 * i + 1)))
                    dst = out[b].rearrange("(t p) d -> p t d", p=P)[:, 2 * i:2 * i + 2, :]
                    sp.dma_start(dst, xs[:, 2 * i:2 * i + 2, :]).then_inc(x_out, 16)
            sp.wait_ge(x_out, 16 * PAIRS * BATCH + 16)

        @block.tensor
        def _(pe):
            pe.wait_ge(ready, READY)
            for s in (nm_turned, xn_turned, qkv_ready, rec_turned, pv_done, o_turned, xc_turned, wo_ready, xd_turned, ffn_ready):
                pe.sem_inc(s.sem, s.credit)

            def turn(src, dst, done):
                for c in range(KC):
                    ins = pe.transpose(dst[:, c * P:(c + 1) * P], src[:, c * P:(c + 1) * P], ident[:])
                ins.then_inc(done.sem, 1)

            def project(xT, w, dst, n0, n1, done=None):
                for c in range(KC):
                    ins = pe.matmul(dst, xT[:, c, :], w[:, c, n0:n1], start=(c == 0), stop=(c == KC - 1))
                if done is not None:
                    ins.then_inc(done.sem, 1)

            def round_(b, l, r):
                def turn_xn(t, k):
                    pe.wait_ge(xn_ready.sem, xn_ready.after(r * (2 * TILES) + t))
                    turn(xn[:, k, :], psE[:, k, :], xn_turned)

                def qkv(t, k):
                    T = r * TILES + t
                    pe.wait_ge(xnT_ready.sem, xnT_ready.after(T))
                    pe.wait_ge(qkv_used.sem, qkv_used.after(T - 2))
                    project(xnT[:, k], wq_s, psM[:, 2 * k, :], 0, DIM)
                    project(xnT[:, k], wq_s, psM[:, 2 * k + 1, 0:QKV - DIM], DIM, QKV, qkv_ready)

                def turn_rec(t, k):
                    T = r * TILES + t
                    pe.wait_ge(rec_ready.sem, rec_ready.after(T))
                    for q in range(5):
                        if q in (0, 3):
                            pe.wait_ge(rec_act.sem, rec_act.after(T * 2 + (-1 if q == 0 else 0)))
                        elif q == 1:
                            pe.wait_ge(rec_dve.sem, rec_dve.after(T * 3 - 1))
                        else:
                            pe.wait_ge(rec_dve.sem, rec_dve.after(T * 3 + (q // 2 - 1)))
                        bank = rec_banks[(k + q) % 2]
                        for h in range(8):
                            src = q_rec[:, k, 8 * q + h] if q < 4 else k_rec[:, k, h]
                            ins = pe.transpose(bank[:, h * P:(h + 1) * P], src.rearrange("p s d -> p (s d)"), ident_b[:])
                        ins.then_inc(rec_turned.sem, 1)

                def body(i, first, last):
                    turn_xn(i * 2 + 1, 1)
                    qkv(i * 2, 0)
                    if not first:
                        turn_rec(i * 2 - 1, 1)
                    if not last:
                        turn_xn(i * 2 + 2, 0)
                    qkv(i * 2 + 1, 1)
                    turn_rec(i * 2, 0)

                pe.wait_ge(wq_in, r * 16 + 16)
                turn_xn(0, 0)
                body(0, True, False)
                with pe.Fori(1, PAIRS - 1) as i:
                    body(i, False, False)
                body(PAIRS - 1, False, True)
                turn_rec(TILES - 1, 1)

                def unit(g, n):
                    M = (r * KV + g) * NU + n
                    qt, heads = UNITS[n]
                    keys = (qt + 1) * P
                    pe.wait_ge(unit_used.sem, unit_used.after(M - 2))
                    banks = psM[:, 2 * (n % 2):2 * (n % 2) + 2, :].rearrange("p a b -> p (a b)")
                    for n_h, h in enumerate(heads):
                        at = n_h * keys if keys != 384 else n_h * 512
                        for k0 in range(0, keys, 512):
                            k1 = min(keys, k0 + 512)
                            diag = k1 == keys
                            ins = pe.matmul(banks[:, at + k0:at + k1], qT[:, g * REP + h, qt * P:(qt + 1) * P],
                                            kT[:, g, k0:k1], start=True, stop=not diag)
                        ins = pe.matmul(banks[:, at + keys - P:at + keys], ident_b[:], tri_b[:], start=False, stop=True)
                    ins.then_inc(unit_ready.sem, 1)

                def nm_turn(g, c):
                    n = (r * KV + g) * CHUNKS + c
                    pe.wait_ge(nm_split.sem, nm_split.after(n))
                    for qt in range(QT_PER_CHUNK):
                        ins = pe.transpose(nm_ps[0:3 * REP, qt * P:(qt + 1) * P],
                                           nm_parts[:, c, qt].rearrange("p a h -> p (a h)"), ident_b[:])
                    ins.then_inc(nm_turned.sem, 1)

                def scores(g, s):
                    c, kb, q0, w = STEPS[s]
                    if s in (0, FIRST_1):
                        pe.wait_ge(nm_in[c], (r * KV + g) * 16 + 32)
                    for j in range(REP):
                        e = ((r * KV + g) * NS + s) * REP + j
                        pe.wait_ge(p_ready.sem, p_ready.after(e - 2))
                        pe.matmul(psE[:, j % 2, 0:w], kT[:, g, kb * P:(kb + 1) * P],
                                  qT[:, g * REP + j, q0:q0 + w], start=True, stop=True).then_inc(st_ready.sem, 1)

                def pv(g, s):
                    c, kb, q0, w = STEPS[s]
                    u = r * KV + g
                    off = q0 - c * QCHUNK
                    if s == 0:
                        pe.wait_ge(v_ready.sem, v_ready.after(u))
                    if kb == 0:
                        pe.wait_ge(o_copied.sem, o_copied.after(u * CHUNKS + (c - 1)))
                    if kb >= c * QT_PER_CHUNK:
                        pe.wait_ge(masked.sem, masked.after(u * ND + kb))
                    else:
                        pe.wait_ge(p_ready.sem, p_ready.after((u * NS + s) * REP + (REP - 1)))
                    for j in range(REP):
                        ins = pe.matmul(psO[VW * j:VW * (j + 1), off:off + w], v_grp[:, kb, :],
                                        probs[:, s % PSLOTS, j, 0:w], start=(kb == 0),
                                        stop=(kb == (c + 1) * QT_PER_CHUNK - 1), tile_position=(0, VW * j))
                    ins.then_inc(pv_done.sem, 1)

                def o_turn(g, c):
                    n = (r * KV + g) * CHUNKS + c
                    pe.wait_ge(o_copied.sem, o_copied.after(n))
                    turn(o_T[:, c, :], psT[:], o_turned)

                def psT_free(g, what):
                    u = r * KV + g
                    nms, outs = {"N1": (1, -1), "O-1": (2, -1), "N0": (2, 0), "O0": (3, 0), "O0last": (2, 0),
                                 "first": (0, 0), "first1": (1, 0), "Olast": (2, 1)}[what]
                    return nms, outs

                def group(g, has_prev, has_next):
                    u = r * KV + g
                    for what, *arg in group_order(has_prev, has_next):
                        if what == "S":
                            scores(g, arg[0])
                        elif what == "U":
                            unit(g + 1, arg[0])
                        elif what == "PV":
                            pv(g, arg[0])
                        elif what == "N":
                            c, d = arg
                            outs = u * CHUNKS - 1 if c == 1 else u * CHUNKS
                            if c == 1 and not has_prev:
                                outs = u * CHUNKS
                            pe.wait_ge(o_done.sem, o_done.after(outs - 1))
                            if not (c == 0 and d == 0):
                                pe.wait_ge(nm_copied.sem, nm_copied.after((u + d) * CHUNKS + (c - 1)))
                            nm_turn(g + d, c)
                        elif what == "O":
                            c, d = arg
                            pe.wait_ge(nm_copied.sem, nm_copied.after(
                                (u + 1) * CHUNKS if (c == 0 and has_next) else u * CHUNKS + 1))
                            pe.wait_ge(o_done.sem, o_done.after((u + d) * CHUNKS + (c - 1)))
                            o_turn(g + d, c)

                pe.wait_ge(rec_act.sem, rec_act.after(r * (2 * TILES) + (2 * TILES - 1)))
                pe.wait_ge(rec_dve.sem, rec_dve.after(r * (3 * TILES) + (3 * TILES - 1)))
                for n in range(UNITS_0):
                    unit(0, n)
                nm_turn(0, 0)
                for n in range(UNITS_0, NU):
                    unit(0, n)
                group(0, False, True)
                with pe.Fori(1, KV - 1) as g:
                    group(g, True, True)
                group(KV - 1, True, False)
                pe.wait_ge(o_done.sem, o_done.after((r * KV + KV - 1) * CHUNKS))
                o_turn(KV - 1, 1)

                def cd(i, has_c, has_d):
                    def C(k):
                        return r * TILES + i * 2 + k

                    def D(k):
                        return r * TILES + i * 2 + (k - 2)
                    if has_c:
                        for k in range(2):
                            pe.wait_ge(xc_ready.sem, xc_ready.after(C(k)))
                            turn(xc[:, k, :], psE[:, k, :], xc_turned)
                    if has_d:
                        for k in range(2):
                            pe.wait_ge(xn_ready.sem, xn_ready.after(r * (2 * TILES) + (TILES - 2) + i * 2 + k))
                            turn(xn[:, k, :], (psT if k == 0 else psO)[:], xd_turned)
                    if has_c:
                        for k in range(2):
                            pe.wait_ge(xcT_ready.sem, xcT_ready.after(C(k)))
                            pe.wait_ge(wo_added.sem, wo_added.after(C(k) - 2))
                            project(xcT[:, k], wo_s, psM[:, k, :], 0, DIM, wo_ready)
                    if has_d:
                        for k in range(2):
                            pe.wait_ge(xdT_ready.sem, xdT_ready.after(D(k)))
                            pe.wait_ge(ffn_added.sem, ffn_added.after(D(k) - 2))
                            project(xnT[:, k], wf_s, psM[:, 2 + k, :], 0, DIM, ffn_ready)

                pe.wait_ge(wo_in, r * 16 + 16)
                cd(0, True, False)
                with pe.Fori(1, PAIRS) as i:
                    cd(i, True, True)
                cd(PAIRS, False, True)

            rounds(pe, round_)

        @block.scalar
        def _(act):
            act.wait_ge(ready, READY)
            for s in (qkv_used, rec_act, p_ready, o_copied):
                act.sem_inc(s.sem, s.credit)

            def first_rstd(q):
                act.wait_ge(var_ready.sem, var_ready.after(q))
                act.activation(ln_var[:], mv[:, :, 1], ACT.Ln, bias=eps_s[:, 0:1]).then_inc(ln_done.sem, 1)
                act.wait_ge(ln_done.sem, ln_done.after(q))
                act.activation(rs0[:], ln_var[:], ACT.Exp, scale=-0.5).then_inc(rs_ready.sem, 1)

            def copy_T(dst, src, done):
                act.activation(dst.rearrange("p a b -> p (a b)"), src, ACT.Copy).then_inc(done.sem, 1)

            def round_(b, l, r):
                def xn_T(t, k):
                    act.wait_ge(xn_turned.sem, xn_turned.after(r * TILES + t))
                    act.wait_ge(qkv_ready.sem, qkv_ready.after(r * TILES + t - 2))
                    copy_T(xnT[:, k], psE[:, k, :], xnT_ready)

                def rec_copy(t, k):
                    for q in (1, 3):
                        act.wait_ge(rec_turned.sem, rec_turned.after((r * TILES + t) * 5 + q))
                        act.activation(qT[:, 8 * q:8 * q + 8, bass.ds(t * P, P)],
                                       rec_banks[(k + q) % 2].rearrange("p (h n) -> p h n", h=8),
                                       ACT.Copy).then_inc(rec_act.sem, 1)

                def parts(t, k):
                    T = r * TILES + t
                    act.wait_ge(qkv_ready.sem, qkv_ready.after(T))
                    act.activation(qk[:, k, 0:DIM], psM[:, 2 * k, :], ACT.Copy)
                    act.activation(qk[:, k, DIM:QK], psM[:, 2 * k + 1, 0:QK - DIM], ACT.Copy).then_inc(qk_ready.sem, 1)
                    act.activation(vs[:, bass.ds(t, 1), :, 0:HD].rearrange("p a h d -> p (a h) d"),
                                   psM[:, 2 * k + 1, QK - DIM:QKV - DIM].rearrange("p (h d) -> p h d", d=HD),
                                   ACT.Copy).then_inc(qkv_used.sem, 1)
                    rq = r_s[:, k, 0:DIM].rearrange("p (h a d) -> p h a d", h=HEADS, a=1)
                    rk = r_s[:, k, DIM:QK].rearrange("p (h a d) -> p h a d", h=KV, a=1)
                    tq = t_s[:, k, 0:DIM].rearrange("p (h a d) -> p h a d", h=HEADS, a=1)
                    tk = t_s[:, k, DIM:QK].rearrange("p (h a d) -> p h a d", h=KV, a=1)
                    act.wait_ge(rec_turned.sem, rec_turned.after(T * 5 - 6))
                    act.wait_ge(rope_ready.sem, rope_ready.after(T))
                    act.activation(q_rec[:, k, :, 0:3, :], rq.to_broadcast([P, HEADS, 3, HD]), ACT.Copy)
                    act.activation(k_rec[:, k, :, 1:6:2, :], rk.to_broadcast([P, KV, 3, HD]), ACT.Copy).then_inc(h_ready.sem, 1)
                    act.wait_ge(r1_ready.sem, r1_ready.after(T))
                    act.activation(q_rec[:, k, :, 3:5, :], tq.to_broadcast([P, HEADS, 2, HD]), ACT.Copy)
                    act.activation(k_rec[:, k, :, 2:7:2, :], tk.to_broadcast([P, KV, 3, HD]), ACT.Copy).then_inc(m_ready.sem, 1)

                def body(i, first, last):
                    xn_T(i * 2 + 1, 1)
                    if not first:
                        rec_copy(i * 2 - 1, 1)
                    parts(i * 2, 0)
                    if not last:
                        first_rstd(r * (2 * PAIRS) + i + 1)
                        xn_T(i * 2 + 2, 0)
                    rec_copy(i * 2, 0)
                    parts(i * 2 + 1, 1)

                first_rstd(r * (2 * PAIRS))
                xn_T(0, 0)
                body(0, True, False)
                with act.Fori(1, PAIRS - 1) as i:
                    body(i, False, False)
                body(PAIRS - 1, False, True)
                rec_copy(TILES - 1, 1)

                def exps(g, s):
                    w = STEPS[s][3]
                    step = (r * KV + g) * NS + s
                    act.wait_ge(pv_done.sem, pv_done.after(step - PSLOTS))
                    for j in range(REP):
                        act.wait_ge(st_ready.sem, st_ready.after(step * REP + j))
                        act.activation(probs[:, s % PSLOTS, j, 0:w], psE[:, j % 2, 0:w], ACT.Exp).then_inc(p_ready.sem, 1)

                def o_copy(g, c):
                    n = (r * KV + g) * CHUNKS + c
                    last_step = FIRST_1 - 1 if c == 0 else NS - 1
                    act.wait_ge(pv_done.sem, pv_done.after((r * KV + g) * NS + last_step))
                    act.wait_ge(o_turned.sem, o_turned.after(n - CHUNKS))
                    act.activation(o_T[:, c, :], psO[:], ACT.Copy).then_inc(o_copied.sem, 1)

                with act.Fori(0, KV) as g:
                    for s in range(NS):
                        exps(g, s)
                        if s == FIRST_1 + 1:
                            o_copy(g, 0)
                    o_copy(g, 1)

                def cd(i, has_c, has_d):
                    if has_c:
                        for k in range(2):
                            n = r * TILES + i * 2 + k
                            act.wait_ge(xc_turned.sem, xc_turned.after(n))
                            act.wait_ge(wo_ready.sem, wo_ready.after(n - 2))
                            copy_T(xcT[:, k], psE[:, k, :], xcT_ready)
                    if has_d:
                        for k in range(2):
                            n = r * TILES + i * 2 + (k - 2)
                            act.wait_ge(xd_turned.sem, xd_turned.after(n))
                            act.wait_ge(ffn_ready.sem, ffn_ready.after(n - 2))
                            copy_T(xnT[:, k], (psT if k == 0 else psO)[:], xdT_ready)
                    if has_c:
                        first_rstd(r * (2 * PAIRS) + PAIRS + i)

                cd(0, True, False)
                with act.Fori(1, PAIRS) as i:
                    cd(i, True, True)
                cd(PAIRS, False, True)

            rounds(act, round_)

        @block.vector
        def _(dve):
            dve.memset(eps_s[:], EPS)
            dve.memset(vs[:, :, :, HD:VW], 0.0)
            dve.memset(k_rec[:, :, :, SLOTS - 1, :], 0.0).then_inc(ready, 1)
            dve.wait_ge(ready, 1)
            dve.memset(vs[:, :, :, HD:HD + 1], 1.0)
            dve.memset(k_rec[:, :, :, SLOTS - 1, 0:3], 1.0).then_inc(ready, 1)
            dve.wait_ge(consts_in, 16 * 6)
            dve.tensor_copy(ident_b[:], ident[:])
            dve.tensor_copy(tri_b[:], rows[:, 0:P])
            dve.tensor_copy(wf_s[:], wf_raw[:]).then_inc(ready, 1)
            dve.wait_ge(ready, 3)
            dve.tensor_scalar(wf_s[:], wf_s[:], 2.0, -1.0, ALU.mult, ALU.add).then_inc(ready, 1)
            for s in (rec_ready, rec_dve, unit_used, o_done, wo_added, ffn_added):
                dve.sem_inc(s.sem, s.credit)

            def layer_norm(q, i, t_base):
                links = [0]

                def link(ins):
                    ins.then_inc(ln_self.sem, 1)
                    wait_alone(dve, ln_self.sem, ln_self.after(q * LN_LINKS + links[0]))
                    links[0] += 1

                for k in range(2):
                    ins = dve.bn_stats(stats[:, k, :], xs[:, bass.ds(i * 2 + k, 1), :].rearrange("p a d -> p (a d)"))
                link(ins)
                dve.bn_aggr(mv[:, 0, :], stats[:, 0, :])
                dve.bn_aggr(mv[:, 1, :], stats[:, 1, :]).then_inc(var_ready.sem, 1)
                dve.wait_ge(var_ready.sem, var_ready.after(q))
                link(dve.tensor_scalar(var_eps[:], mv[:, :, 1], EPS, None, ALU.add))
                dve.wait_ge(rs_ready.sem, rs_ready.after(q))
                link(dve.tensor_tensor(newton[:], rs0[:], rs0[:], ALU.mult))
                link(dve.tensor_tensor(newton2[:], newton[:], var_eps[:], ALU.mult))
                link(dve.tensor_scalar(newton[:], newton2[:], -0.5, 1.5, ALU.mult, ALU.add))
                link(dve.tensor_tensor(rstd[:], rs0[:], newton[:], ALU.mult))
                assert links[0] == LN_LINKS
                for k in range(2):
                    dve.tensor_scalar(xn[:, k, :], xs[:, bass.ds(i * 2 + k, 1), :].rearrange("p a d -> p (a d)"),
                                      mv[:, k, 0:1], rstd[:, k:k + 1], ALU.subtract, ALU.mult).then_inc(xn_ready.sem, 1)

            def round_(b, l, r):
                def ln_a(i):
                    dve.wait_ge(ffn_added.sem, ffn_added.after(r * TILES - TILES + i * 2 + 1))
                    wait_alone(dve, xn_turned.sem, xn_turned.after(r * TILES + i * 2 - 1))
                    layer_norm(r * (2 * PAIRS) + i, i, 0)

                def rec_copy(t, k):
                    for q in (0, 2, 4):
                        dve.wait_ge(rec_turned.sem, rec_turned.after((r * TILES + t) * 5 + q))
                        to = qT[:, 8 * q:8 * q + 8, bass.ds(t * P, P)] if q < 4 else kT[:, :, bass.ds(t * P, P)]
                        dve.tensor_copy(to, rec_banks[(k + q) % 2].rearrange("p (h n) -> p h n", h=8)).then_inc(rec_dve.sem, 1)

                def parts(t, k):
                    T = r * TILES + t
                    dve.wait_ge(qk_ready.sem, qk_ready.after(T))
                    c = cos_s[:, bass.ds(l, 1), bass.ds(t, 1), :].rearrange("p a b d -> p (a b) d")
                    dve.tensor_tensor(r_s[:, k].rearrange("p (h d) -> p h d", d=HD),
                                      qk[:, k].rearrange("p (h d) -> p h d", d=HD),
                                      c.to_broadcast([P, HEADS + KV, HD]), ALU.mult).then_inc(cos_self.sem, 1)
                    dve.wait_ge(cos_self.sem, cos_self.after(T))
                    dve.wait_ge(sin_ready.sem, sin_ready.after(T))
                    dve.tensor_tensor(r_s[:, k], r_s[:, k], t_s[:, k], ALU.add).then_inc(rope_ready.sem, 1)
                    dve.wait_ge(m_ready.sem, m_ready.after(T))
                    tq = t_s[:, k, 0:DIM].rearrange("p (h a d) -> p h a d", h=HEADS, a=1)
                    tk = t_s[:, k, DIM:QK].rearrange("p (h d) -> p h d", h=KV)
                    dve.tensor_tensor(q_rec[:, k, :, 5:7, :], tq.to_broadcast([P, HEADS, 2, HD]),
                                      q_rec[:, k, :, 3:5, :], ALU.subtract)
                    dve.tensor_tensor(k_rec[:, k, :, 0, :], tk, k_rec[:, k, :, 2, :], ALU.subtract).then_inc(rec_ready.sem, 1)

                def body(i, first, last):
                    if not first:
                        rec_copy(i * 2 - 1, 1)
                    parts(i * 2, 0)
                    if not last:
                        ln_a(i + 1)
                    rec_copy(i * 2, 0)
                    parts(i * 2 + 1, 1)

                for i in range(PAIRS):
                    dve.wait_ge(x_in[i], b * 16 + 16)
                ln_a(0)
                body(0, True, False)
                with dve.Fori(1, PAIRS - 1) as i:
                    body(i, False, False)
                body(PAIRS - 1, False, True)
                rec_copy(TILES - 1, 1)

                def unit(g, n):
                    M = (r * KV + g) * NU + n
                    qt, heads = UNITS[n]
                    keys = (qt + 1) * P
                    if n in (0, UNITS_0):
                        dve.wait_ge(nm_split.sem, nm_split.after((r * KV + g - 1) * CHUNKS + (0 if n == 0 else 1)))
                    dve.wait_ge(unit_ready.sem, unit_ready.after(M))
                    banks = psM[:, 2 * (n % 2):2 * (n % 2) + 2, :].rearrange("p a b -> p (a b)")
                    pitch = keys if keys != 384 else 512
                    src = banks[:, 0:pitch * len(heads)].rearrange("p (h k) -> p h k", k=pitch)[:, :, 0:keys]
                    dve.tensor_reduce(mx[:, qt, heads[0]:heads[0] + len(heads)], src, AX.X, ALU.max).then_inc(unit_used.sem, 1)

                def nm_copy(g, c):
                    u = r * KV + g
                    dve.wait_ge(nm_turned.sem, nm_turned.after(u * CHUNKS + c))
                    dve.wait_ge(nm_in[c], u * 16 + 16)
                    dve.tensor_copy(nm_rows[:, c, :], nm_ps[0:3 * REP, 0:QCHUNK]).then_inc(nm_copied.sem, 1)

                def o_divide(g, c):
                    n = (r * KV + g) * CHUNKS + c
                    dve.wait_ge(o_turned.sem, o_turned.after(n))
                    o = psT[:].rearrange("p (t h d) -> p t h d", t=QT_PER_CHUNK, h=REP)
                    dve.reciprocal(den[:], o[:, :, :, HD]).then_inc(o_self.sem, 1)
                    dve.wait_ge(o_self.sem, o_self.after(n))
                    to = attn[:, c * QT_PER_CHUNK:(c + 1) * QT_PER_CHUNK, bass.ds(g * (REP * HD), REP * HD)]
                    dve.tensor_tensor(to.rearrange("p t (h d) -> p t h d", h=REP), o[:, :, :, 0:HD],
                                      den[:].rearrange("p t (h a) -> p t h a", a=1).to_broadcast([P, QT_PER_CHUNK, REP, HD]),
                                      ALU.mult).then_inc(o_done.sem, 1)

                def group(g, has_prev, has_next):
                    for what, *arg in group_order(has_prev, has_next):
                        if what == "U":
                            unit(g + 1, arg[0])
                        elif what == "N":
                            nm_copy(g + arg[1], arg[0])
                        elif what == "O":
                            o_divide(g + arg[1], arg[0])

                for n in range(UNITS_0):
                    unit(0, n)
                nm_copy(0, 0)
                for n in range(UNITS_0, NU):
                    unit(0, n)
                group(0, False, True)
                with dve.Fori(1, KV - 1) as g:
                    group(g, True, True)
                group(KV - 1, True, False)
                o_divide(KV - 1, 1)

                def add_wo(i, k):
                    n = r * TILES + i * 2 + k
                    dve.wait_ge(wo_ready.sem, wo_ready.after(n))
                    xt = xs[:, bass.ds(i * 2 + k, 1), :].rearrange("p a d -> p (a d)")
                    dve.tensor_tensor(xt, psM[:, k, :], xt, ALU.add).then_inc(wo_added.sem, 1)

                def add_ffn(i, k):
                    n = r * TILES + i * 2 + (k - 2)
                    dve.wait_ge(ffn_ready.sem, ffn_ready.after(n))
                    xt = xs[:, bass.ds(i * 2 + (k - 2), 1), :].rearrange("p a d -> p (a d)")
                    dve.scalar_tensor_tensor(out=xt, in0=psM[:, 2 + k, :], scalar=scale_s[:, 0:1], in1=xt,
                                             op0=ALU.mult, op1=ALU.add).then_inc(ffn_added.sem, 1)

                def cd(i, has_c, has_d):
                    if has_c:
                        for k in range(2):
                            add_wo(i, k)
                        dve.wait_ge(wo_added.sem, wo_added.after(r * TILES + i * 2 + 1))
                        wait_alone(dve, xd_turned.sem, xd_turned.after(r * TILES + i * 2 - 1))
                        layer_norm(r * (2 * PAIRS) + PAIRS + i, i, TILES)
                    if has_d:
                        for k in range(2):
                            add_ffn(i, k)

                cd(0, True, False)
                with dve.Fori(1, PAIRS) as i:
                    cd(i, True, True)
                cd(PAIRS, False, True)

            rounds(dve, round_)

        @block.gpsimd
        def _(pool):
            pool.wait_ge(ready, READY)
            pool.sem_inc(nm_split.sem, nm_split.credit)

            def round_(b, l, r):
                def parts(t, k):
                    T = r * TILES + t
                    wait_alone(pool, qk_ready.sem, qk_ready.after(T))
                    wait_alone(pool, rec_ready.sem, rec_ready.after(T - 2))
                    x4 = qk[:, k].rearrange("p (h a d) -> p h a d", a=2, d=HALF)
                    t4 = t_s[:, k].rearrange("p (h a d) -> p h a d", a=2, d=HALF)
                    sn = sin_s[:, bass.ds(l, 1), bass.ds(t, 1), :].rearrange("p a b d -> p (a b) d")
                    for a in range(2):
                        ins = pool.tensor_tensor(t4[:, :, a, :], x4[:, :, 1 - a, :],
                                                 sn[:, :, a * HALF:(a + 1) * HALF].to_broadcast([P, HEADS + KV, HALF]), ALU.mult)
                    ins.then_inc(sin_ready.sem, 1)
                    wait_alone(pool, rec_turned.sem, rec_turned.after(T * 5 - 6))
                    pool.memset(q_rec[:, k, :, SLOTS - 1, :], 0.0)
                    wait_alone(pool, h_ready.sem, h_ready.after(T))
                    rq = r_s[:, k, 0:DIM].rearrange("p (h d) -> p h d", d=HD)
                    rk = r_s[:, k, DIM:QK].rearrange("p (h d) -> p h d", d=HD)
                    tq = t_s[:, k, 0:DIM].rearrange("p (h d) -> p h d", d=HD)
                    tk = t_s[:, k, DIM:QK].rearrange("p (h d) -> p h d", d=HD)
                    pool.tensor_tensor(tq, rq, q_rec[:, k, :, 0, :], ALU.subtract)
                    pool.tensor_tensor(tk, rk, k_rec[:, k, :, 1, :], ALU.subtract).then_inc(r1_ready.sem, 1)

                with pool.Fori(0, PAIRS) as i:
                    parts(i * 2, 0)
                    parts(i * 2 + 1, 1)

                def nm_parts_of(g, c):
                    n = (r * KV + g) * CHUNKS + c
                    links = [0]

                    def link(ins):
                        ins.then_inc(nm_self.sem, 1)
                        wait_alone(pool, nm_self.sem, nm_self.after(n * NM_LINKS + links[0]))
                        links[0] += 1

                    last_unit = UNITS_0 - 1 if c == 0 else NU - 1
                    wait_alone(pool, unit_used.sem, unit_used.after((r * KV + g) * NU + last_unit))
                    wait_alone(pool, nm_turned.sem, nm_turned.after(n - 2))
                    link(pool.tensor_scalar(nm[:], mx[:, c * QT_PER_CHUNK:(c + 1) * QT_PER_CHUNK, :], -1.0, None, ALU.mult))
                    link(pool.tensor_copy(nm_parts[:, c, :, 0, :], nm[:]))
                    link(pool.tensor_tensor(nm_r[:], nm[:], nm_parts[:, c, :, 0, :], ALU.subtract))
                    link(pool.tensor_copy(nm_parts[:, c, :, 1, :], nm_r[:]))
                    pool.tensor_tensor(nm_parts[:, c, :, 2, :], nm_r[:], nm_parts[:, c, :, 1, :], ALU.subtract).then_inc(nm_split.sem, 1)
                    assert links[0] == NM_LINKS

                def mask(g, s):
                    u = r * KV + g
                    wait_alone(pool, p_ready.sem, p_ready.after((u * NS + s) * REP + (REP - 1)))
                    d = probs[:, s % PSLOTS, :, 0:P]
                    pool.affine_select(out=d, in_=d, compare_op=ALU.is_ge, fill=0.0, base=0,
                                       pattern=[[0, REP], [1, P]], channel_multiplier=-1).then_inc(masked.sem, 1)

                def group(g, has_next):
                    u = r * KV + g
                    wait_alone(pool, pv_done.sem, pv_done.after(u * NS - 1))
                    pool.tensor_copy(v_grp[:], vs[:, :, bass.ds(g, 1), :].rearrange("p t a d -> p t (a d)")).then_inc(v_ready.sem, 1)
                    for s in range(FIRST_1):
                        mask(g, s)
                    if has_next:
                        nm_parts_of(g + 1, 0)
                    for s in range(NS - QT_PER_CHUNK, NS):
                        mask(g, s)
                    if has_next:
                        nm_parts_of(g + 1, 1)

                nm_parts_of(0, 0)
                nm_parts_of(0, 1)
                with pool.Fori(0, KV - 1) as g:
                    group(g, True)
                group(KV - 1, False)

                def tile_out(t, k):
                    n = r * TILES + t
                    wait_alone(pool, xc_turned.sem, xc_turned.after(n - 2))
                    pool.tensor_copy(xc[:, k, :], attn[:, bass.ds(t, 1), :].rearrange("p a d -> p (a d)")).then_inc(xc_ready.sem, 1)

                wait_alone(pool, o_done.sem, o_done.after((r * KV + KV - 1) * CHUNKS + 1))
                with pool.Fori(0, PAIRS) as i:
                    tile_out(i * 2, 0)
                    tile_out(i * 2 + 1, 1)

            rounds(pool, round_)


def tables():
    import numpy as np
    cos, sin = [], []
    for base in (10000.0, 500000.0):
        inv = (np.float32(1.0) / np.power(np.float32(base), np.arange(0, HD, 2, dtype=np.float32) / np.float32(HD))).astype(np.float32)
        ang = (np.arange(SEQ, dtype=np.float32)[:, None] * inv[None, :]).astype(np.float64)
        c, s = 0.5 * np.cos(ang), 0.5 * np.sin(ang)
        cos.append(np.concatenate([c, c], 1))
        sin.append(np.concatenate([-s, s], 1))
    shape = lambda a: np.ascontiguousarray(np.stack(a).astype(np.float32).reshape(LAYERS, TILES, P, HD).transpose(2, 0, 1, 3))
    return shape(cos), shape(sin)


def kernel(L0_attn_a_x, L0_attn_a_w_qkv, L0_attn_a_w_o, L0_attn_b_w_qkv, L0_attn_b_w_o, L0_ffn_kernel, L0_ffn_scale):
    import numpy as np
    import concourse.bacc as bacc
    from concourse.bass_utils import run_bass_kernel_spmd

    wa = np.asarray(L0_attn_a_w_qkv)
    wa_qk = wa[:, :QK].reshape(DIM, QK // HD, HALF, 2).transpose(0, 1, 3, 2).reshape(DIM, QK)
    wa = np.concatenate([wa_qk, wa[:, QK:]], 1)
    wb = np.asarray(L0_attn_b_w_qkv).T
    cos, sin = tables()
    tri = np.where(np.arange(P)[None, :] > np.arange(P)[:, None], np.float32(-1e30), np.float32(0)).astype(np.float32)
    arrays = {
        "x": np.ascontiguousarray(L0_attn_a_x),
        "w_qkv": np.ascontiguousarray(np.stack([wa, wb])),
        "w_o": np.ascontiguousarray(np.stack([np.asarray(L0_attn_a_w_o), np.asarray(L0_attn_b_w_o).T])),
        "w_ffn": np.ascontiguousarray(L0_ffn_kernel),
        "scale": np.ascontiguousarray(np.asarray(L0_ffn_scale).reshape(1)),
        "cos": cos,
        "sin": sin,
        "eye": np.eye(P, dtype=np.float32),
        "tri": tri,
    }
    nc = bacc.Bacc("TRN2", target_bir_lowering=False, num_devices=1)
    args = [nc.dram_tensor(f"in_{n}", a.shape, mybir.dt.from_np(a.dtype), kind="ExternalInput").ap() for n, a in arrays.items()]
    out = nc.dram_tensor("out_x", (BATCH, SEQ, DIM), F32, kind="ExternalOutput").ap()
    build(nc, *args, out)
    res = run_bass_kernel_spmd(nc, [{f"in_{n}": a for n, a in arrays.items()}], core_ids=[0])
    return res.results[0]["out_x"]
```

```python
from contextlib import ExitStack

import concourse.bass as bass
from concourse import mybir

ALU = mybir.AluOpType
ACT = mybir.ActivationFunctionType
AX = mybir.AxisListType
F32 = mybir.dt.float32
BF16 = mybir.dt.bfloat16
U8 = mybir.dt.uint8

P = 128
SEQ = 1024
DIM = 512
HEADS = 32
KV = 8
REP = HEADS // KV
HD = DIM // HEADS
HALF = HD // 2
BATCH = 2
LAYERS = 2
EPS = 1e-5

TILES = SEQ // P
PAIRS = TILES // 2
KC = DIM // P
QKV = DIM + 2 * KV * HD
QK = DIM + KV * HD
QCHUNK = 512
CHUNKS = SEQ // QCHUNK
QT_PER_CHUNK = QCHUNK // P
VW = 32
PSLOTS = 3

SLOTS = 8
MAXROW = (SLOTS - 1) * HD
DEPTH = MAXROW + 3
RECS = 3


class Signal:

    def __init__(self, sem, credit=0):
        self.sem, self.credit = sem, credit

    def after(self, n):
        return n + (self.credit + 1)


def score_steps():
    out = []
    for c in range(CHUNKS):
        before = list(range(c * QT_PER_CHUNK))
        diagonal = list(range(c * QT_PER_CHUNK, (c + 1) * QT_PER_CHUNK))
        order = [kb for pair in zip(before, diagonal) for kb in pair] if before else diagonal
        for kb in order:
            q0 = max(c * QCHUNK, kb * P)
            out.append((c, kb, q0, (c + 1) * QCHUNK - q0))
    return out


def head_batches(step):
    per = max(1, QCHUNK // step[3])
    return [list(range(h, min(REP, h + per))) for h in range(0, REP, per)]


def last_exp(s):
    return EXPS_BEFORE[s] + len(head_batches(STEPS[s])) - 1


def max_units():
    out = []
    for qt in range(TILES):
        keys = (qt + 1) * P
        per = max(1, 2 * (QCHUNK // keys)) if keys <= QCHUNK else 1
        per = min(per, REP)
        out += [(qt, list(range(h, h + per))) for h in range(0, REP, per)]
    return out


STEPS = score_steps()
UNITS = max_units()
NS = len(STEPS)
NU = len(UNITS)
ND = TILES
UNITS_0 = sum(1 for qt, _ in UNITS if qt < QT_PER_CHUNK)
DIAGONAL = [s for s, (c, kb, q0, w) in enumerate(STEPS) if kb >= c * QT_PER_CHUNK]
SPLIT_AFTER = 5
FIRST_1 = QT_PER_CHUNK
EXPS_BEFORE = [sum(len(head_batches(t)) for t in STEPS[:s]) for s in range(NS)]
NE = sum(len(head_batches(t)) for t in STEPS)
assert NE % 2 == 0 and NS % PSLOTS == 0 and NU % 2 == 0


GROUP_ORDER = """
S.0.0 U.0 S.0.1 U.1 S.0.2 S.0.3 U.2
S.1.0 N.1.0 U.3 S.1.1 S.1.2 U.4 S.1.3 PV.0
S.2.0 U.5 S.2.1 PV.1
S.3.0 U.6
S.4.0 O.1.-1 S.4.1 U.7 S.4.2 U.8 S.4.3 PV.2
S.5.0 U.9 S.5.1 U.10 S.5.2 PV.3 S.5.3 U.11
S.6.0 U.12 S.6.1 PV.4 S.6.2 S.6.3 U.13 U.14 N.0.1
S.7.0 S.7.1 PV.5 S.7.2 S.7.3 U.15 U.16
S.8.0 S.8.1 PV.6 S.8.2 S.8.3 U.17 U.18
S.9.0 S.9.1 PV.7 O.0.0
S.10.0 S.10.1 U.19 U.20 S.10.2 S.10.3 PV.8
S.11.0 PV.9 U.21 PV.10 PV.11
"""


def group_order(has_prev, has_next):
    out = []
    for word in GROUP_ORDER.split():
        what, *arg = word.split(".")
        arg = tuple(int(a) for a in arg)
        if what == "O" and arg[1] < 0 and not has_prev:
            continue
        if not has_next and (what == "U" or (what == "N" and arg[1] > 0)):
            continue
        out.append((what, *arg))
    return out


READY = 4
LN_LINKS = 6
NM_LINKS = 4


def build(nc, x, w_qkv, w_o, w_ffn, scale, cos, sin, eye, tri, out):
    with ExitStack() as ctx:
        def sb(name, shape, dt=F32):
            return ctx.enter_context(nc.sbuf_tensor(name, shape, dt))

        def ps(name, shape, dt=F32):
            return ctx.enter_context(nc.psum_tensor(name, shape, dt))

        def sem(name):
            return ctx.enter_context(nc.semaphore(name))

        xs = sb("xs", [P, TILES, DIM])
        wq_s = sb("wq_s", [P, KC, QKV])
        wo_s = sb("wo_s", [P, KC, DIM])
        wf_s = sb("wf_s", [P, KC, DIM])
        cos_s = sb("cos_s", [P, LAYERS, TILES, HD])
        sin_s = sb("sin_s", [P, LAYERS, TILES, HD])
        ident = sb("ident", [P, P])
        ident_b = sb("ident_b", [P, P], BF16)
        tri_b = sb("tri_b", [P, P], BF16)
        scale_s = sb("scale_s", [P, 1])
        eps_s = sb("eps_s", [P, 1])

        stats = sb("stats", [P, 2, 6])
        mv = sb("mv", [P, 2, 2])
        var_eps = sb("var_eps", [P, 2])
        ln_var = sb("ln_var", [P, 2])
        rs0 = sb("rs0", [P, 2])
        newton = sb("newton", [P, 2])
        newton2 = sb("newton2", [P, 2])
        rstd = sb("rstd", [P, 2])
        xn = sb("xn", [P, 2, DIM])
        xc = sb("xc", [P, 2, DIM])
        xnT = sb("xnT", [P, 2, KC, P])
        xcT = sb("xcT", [P, 2, KC, P])

        qT = sb("qT", [P, HEADS, SEQ], BF16)
        kT = sb("kT", [P, KV, SEQ], BF16)
        vs = sb("vs", [P, TILES, KV, VW])
        v_grp = sb("v_grp", [P, TILES, VW])
        k_rec = sb("k_rec", [P, RECS, KV, SLOTS, HD], BF16)
        o_T = sb("o_T", [P, CHUNKS, QCHUNK])
        mx = sb("mx", [P, TILES, REP])
        nm = sb("nm", [P, QT_PER_CHUNK, REP])
        nm_r = sb("nm_r", [P, QT_PER_CHUNK, REP])
        nm_parts = sb("nm_parts", [P, CHUNKS, QT_PER_CHUNK, 3, REP], BF16)
        nm_rows = sb("nm_rows", [3 * REP, CHUNKS, QCHUNK], BF16)
        den = sb("den", [P, QT_PER_CHUNK, REP])

        attn = sb("attn", [P, TILES, DIM])
        rows = attn[:].rearrange("p t d -> p (t d)")
        qk = rows[:, 0:2 * QK].rearrange("p (b n) -> p b n", b=2)
        r_s = rows[:, 2 * QK:4 * QK].rearrange("p (b n) -> p b n", b=2)
        t_s = rows[:, 4 * QK:6 * QK].rearrange("p (b n) -> p b n", b=2)
        probs = sb("probs", [P, PSLOTS, REP, QCHUNK])
        q_rec = probs[:].rearrange("p a b c -> p (a b c)").bitcast(BF16).rearrange(
            "p (b h s d) -> p b h s d", b=RECS, h=HEADS, s=SLOTS)
        q_rec_last = probs[:].rearrange("p a b c -> p (a b c)").rearrange(
            "p (r n) -> p r n", n=SLOTS * HD // 2)[:, :, MAXROW // 2:]
        wf_raw = sb("wf_raw", [P, KC, DIM], U8)

        psM = ps("psM", [P, 4, 512])
        psE = ps("psE", [P, 2, 512])
        psO = ps("psO", [P, 512])
        psT = ps("psT", [P, 512])
        rec_banks = [psT[:].bitcast(BF16), psO[:].bitcast(BF16)]
        nm_ps = psT[:].bitcast(BF16)

        consts_in = sem("consts_in")
        ready = sem("ready")
        x_in = [sem(f"x_in{i}") for i in range(PAIRS)]
        x_out = sem("x_out")
        wq_in, wo_in = sem("wq_in"), sem("wo_in")
        ln_self = Signal(sem("ln_self"))
        var_ready = Signal(sem("var_ready"))
        ln_done = Signal(sem("ln_done"))
        rs_ready = Signal(sem("rs_ready"))
        xn_ready = Signal(sem("xn_ready"))
        xn_turned = Signal(sem("xn_turned"), 2)
        xnT_ready = Signal(sem("xnT_ready"))
        qkv_ready = Signal(sem("qkv_ready"), 2)
        qk_ready = Signal(sem("qk_ready"))
        qkv_used = Signal(sem("qkv_used"), 2)
        sin_ready = Signal(sem("sin_ready"))
        cos_self = Signal(sem("cos_self"))
        rope_ready = Signal(sem("rope_ready"))
        h_ready = Signal(sem("h_ready"))
        r1_ready = Signal(sem("r1_ready"))
        m_ready = Signal(sem("m_ready"))
        rec_ready = Signal(sem("rec_ready"), 2)
        rec_turned = Signal(sem("rec_turned"), 5 * RECS)
        rec_dve = Signal(sem("rec_dve"), 3)
        rec_act = Signal(sem("rec_act"), 2)
        unit_ready = Signal(sem("unit_ready"))
        unit_used = Signal(sem("unit_used"), 2)
        nm_split = Signal(sem("nm_split"), 2)
        nm_self = Signal(sem("nm_self"))
        nm_turned = Signal(sem("nm_turned"), 2)
        nm_copied = Signal(sem("nm_copied"))
        nm_in = [sem(f"nm_in{c}") for c in range(CHUNKS)]
        st_ready = Signal(sem("st_ready"))
        p_ready = Signal(sem("p_ready"), 2)
        masked = Signal(sem("masked"))
        v_ready = Signal(sem("v_ready"))
        pv_done = Signal(sem("pv_done"), NS)
        o_copied = Signal(sem("o_copied"), 2)
        o_turned = Signal(sem("o_turned"), 2)
        o_self = Signal(sem("o_self"))
        o_done = Signal(sem("o_done"), 2)
        xc_ready = Signal(sem("xc_ready"))
        xc_turned = Signal(sem("xc_turned"), 2)
        xcT_ready = Signal(sem("xcT_ready"))
        wo_ready = Signal(sem("wo_ready"), 8)
        wo_added = Signal(sem("wo_added"), 2)
        xd_turned = Signal(sem("xd_turned"), 2)
        xdT_ready = Signal(sem("xdT_ready"))
        ffn_ready = Signal(sem("ffn_ready"), 2)
        ffn_added = Signal(sem("ffn_added"), 8)

        block = ctx.enter_context(nc.Block())

        passed = sem("passed")

        def wait_alone(eng, signal, value):
            eng.wait_ge(signal, value)
            eng.sem_inc(passed, 1)

        def rounds(eng, body):
            with eng.Fori(0, BATCH) as b:
                with eng.Fori(0, LAYERS) as l:
                    body(b, l, b * LAYERS + l)

        @block.sync
        def _(sp):
            wv = w_ffn.rearrange("(c p) n -> p c n", p=P)
            sp.dma_start(ident[:], eye).then_inc(consts_in, 16)
            sp.dma_start(wf_raw[:], wv).then_inc(consts_in, 16)
            sp.dma_start(cos_s[:], cos).then_inc(consts_in, 16)
            sp.dma_start(sin_s[:], sin).then_inc(consts_in, 16)
            sp.dma_start(scale_s[:], scale.rearrange("(a b) -> a b", a=1).to_broadcast([P, 1])).then_inc(consts_in, 16)
            sp.dma_start(rows[:, 0:P], tri).then_inc(consts_in, 16)

            for s in (x_out, *nm_in):
                sp.sem_inc(s, 16)

            with sp.Fori(0, BATCH) as b:
                for i in range(PAIRS):
                    sp.wait_ge(x_out, b * (16 * PAIRS) + 16)
                    src = x[b].rearrange("(t p) d -> p t d", p=P)[:, 2 * i:2 * i + 2, :]
                    sp.dma_start(xs[:, 2 * i:2 * i + 2, :], src).then_inc(x_in[i], 16)
                with sp.Fori(0, LAYERS) as l:
                    r = b * LAYERS + l
                    sp.wait_ge(qkv_ready.sem, r * TILES + qkv_ready.credit)
                    sp.dma_start(wq_s[:], w_qkv[l].rearrange("(c p) n -> p c n", p=P)).then_inc(wq_in, 16)
                    sp.wait_ge(wo_ready.sem, r * TILES + wo_ready.credit)
                    sp.dma_start(wo_s[:], w_o[l].rearrange("(c p) n -> p c n", p=P)).then_inc(wo_in, 16)
                    with sp.Fori(0, KV) as g:
                        for c in range(CHUNKS):
                            sp.wait_ge(nm_copied.sem, nm_copied.after((r * KV + g) * CHUNKS + c))
                            sp.dma_start(
                                qT[MAXROW:MAXROW + 3, bass.ds(g * REP, REP), c * QCHUNK:(c + 1) * QCHUNK],
                                nm_rows[:, c, :],
                            ).then_inc(nm_in[c], 16)
                for i in range(PAIRS):
                    sp.wait_ge(ffn_added.sem, ffn_added.after(b * (LAYERS * TILES) + ((LAYERS - 1) * TILES + 2 * i + 1)))
                    dst = out[b].rearrange("(t p) d -> p t d", p=P)[:, 2 * i:2 * i + 2, :]
                    sp.dma_start(dst, xs[:, 2 * i:2 * i + 2, :]).then_inc(x_out, 16)
            sp.wait_ge(x_out, 16 * PAIRS * BATCH + 16)

        @block.tensor
        def _(pe):
            pe.wait_ge(ready, READY)
            for s in (nm_turned, xn_turned, qkv_ready, rec_turned, pv_done, o_turned, xc_turned, wo_ready, xd_turned, ffn_ready):
                pe.sem_inc(s.sem, s.credit)

            def turn(src, dst, done):
                for c in range(KC):
                    ins = pe.transpose(dst[:, c * P:(c + 1) * P], src[:, c * P:(c + 1) * P], ident[:])
                ins.then_inc(done.sem, 1)

            def project(xT, w, dst, n0, n1, done=None):
                for c in range(KC):
                    ins = pe.matmul(dst, xT[:, c, :], w[:, c, n0:n1], start=(c == 0), stop=(c == KC - 1))
                if done is not None:
                    ins.then_inc(done.sem, 1)

            def round_(b, l, r):
                def turn_xn(t, k):
                    pe.wait_ge(xn_ready.sem, xn_ready.after(r * (2 * TILES) + t))
                    turn(xn[:, k, :], psE[:, k, :], xn_turned)

                def qkv(t, k):
                    T = r * TILES + t
                    pe.wait_ge(xnT_ready.sem, xnT_ready.after(T))
                    pe.wait_ge(qkv_used.sem, qkv_used.after(T - 2))
                    project(xnT[:, k], wq_s, psM[:, 2 * k, :], 0, DIM)
                    project(xnT[:, k], wq_s, psM[:, 2 * k + 1, 0:QKV - DIM], DIM, QKV, qkv_ready)

                def turn_rec(t):
                    T = r * TILES + t
                    pe.wait_ge(rec_ready.sem, rec_ready.after(T))
                    for q in range(5):
                        if q in (0, 3):
                            pe.wait_ge(rec_act.sem, rec_act.after(T * 2 + (-1 if q == 0 else 0)))
                        elif q == 1:
                            pe.wait_ge(rec_dve.sem, rec_dve.after(T * 3 - 1))
                        else:
                            pe.wait_ge(rec_dve.sem, rec_dve.after(T * 3 + (q // 2 - 1)))
                        bank = rec_banks[(t + q) % 2]
                        for h in range(8):
                            src = q_rec[:, t % RECS, 8 * q + h] if q < 4 else k_rec[:, t % RECS, h]
                            ins = pe.transpose(bank[:, h * P:(h + 1) * P], src.rearrange("p s d -> p (s d)"), ident_b[:])
                        ins.then_inc(rec_turned.sem, 1)

                pe.wait_ge(wq_in, r * 16 + 16)
                turn_xn(0, 0)
                for n in range(TILES + 3):
                    if n + 1 < TILES:
                        turn_xn(n + 1, (n + 1) % 2)
                    if n >= 3:
                        turn_rec(n - 3)
                    if n < TILES:
                        qkv(n, n % 2)

                def unit(g, n):
                    M = (r * KV + g) * NU + n
                    qt, heads = UNITS[n]
                    keys = (qt + 1) * P
                    pe.wait_ge(unit_used.sem, unit_used.after(M - 2))
                    banks = psM[:, 2 * (n % 2):2 * (n % 2) + 2, :].rearrange("p a b -> p (a b)")
                    for n_h, h in enumerate(heads):
                        at = n_h * keys if keys != 384 else n_h * 512
                        for k0 in range(0, keys, 512):
                            k1 = min(keys, k0 + 512)
                            diag = k1 == keys
                            ins = pe.matmul(banks[:, at + k0:at + k1], qT[0:MAXROW, g * REP + h, qt * P:(qt + 1) * P],
                                            kT[0:MAXROW, g, k0:k1], start=True, stop=not diag)
                        ins = pe.matmul(banks[:, at + keys - P:at + keys], ident_b[:], tri_b[:], start=False, stop=True)
                    ins.then_inc(unit_ready.sem, 1)

                def nm_turn(g, c):
                    n = (r * KV + g) * CHUNKS + c
                    pe.wait_ge(nm_split.sem, nm_split.after(n))
                    for qt in range(QT_PER_CHUNK):
                        ins = pe.transpose(nm_ps[0:3 * REP, qt * P:(qt + 1) * P],
                                           nm_parts[:, c, qt].rearrange("p a h -> p (a h)"), ident_b[:])
                    ins.then_inc(nm_turned.sem, 1)

                def scores(g, s, i):
                    c, kb, q0, w = STEPS[s]
                    if s in (0, FIRST_1) and i == 0:
                        pe.wait_ge(nm_in[c], (r * KV + g) * 16 + 32)
                    n = EXPS_BEFORE[s] + i
                    pe.wait_ge(p_ready.sem, p_ready.after((r * KV + g) * NE + n - 2))
                    for at, j in enumerate(head_batches(STEPS[s])[i]):
                        ins = pe.matmul(psE[:, n % 2, at * w:(at + 1) * w], kT[0:DEPTH, g, kb * P:(kb + 1) * P],
                                        qT[0:DEPTH, g * REP + j, q0:q0 + w], start=True, stop=True)
                    ins.then_inc(st_ready.sem, 1)

                def pv(g, s):
                    c, kb, q0, w = STEPS[s]
                    u = r * KV + g
                    off = q0 - c * QCHUNK
                    if s == 0:
                        pe.wait_ge(v_ready.sem, v_ready.after(u))
                    if kb == 0:
                        pe.wait_ge(o_copied.sem, o_copied.after(u * CHUNKS + (c - 1)))
                    if kb >= c * QT_PER_CHUNK:
                        pe.wait_ge(masked.sem, masked.after(u * ND + kb))
                    else:
                        pe.wait_ge(p_ready.sem, p_ready.after(u * NE + last_exp(s)))
                    for j in range(REP):
                        ins = pe.matmul(psO[VW * j:VW * (j + 1), off:off + w], v_grp[:, kb, :],
                                        probs[:, s % PSLOTS, j, 0:w], start=(kb == 0),
                                        stop=(kb == (c + 1) * QT_PER_CHUNK - 1), tile_position=(0, VW * j))
                    ins.then_inc(pv_done.sem, 1)

                def o_turn(g, c):
                    n = (r * KV + g) * CHUNKS + c
                    pe.wait_ge(o_copied.sem, o_copied.after(n))
                    turn(o_T[:, c, :], psT[:], o_turned)

                def group(g, has_prev, has_next):
                    u = r * KV + g
                    for what, *arg in group_order(has_prev, has_next):
                        if what == "S":
                            scores(g, *arg)
                        elif what == "U":
                            unit(g + 1, arg[0])
                        elif what == "PV":
                            pv(g, arg[0])
                        elif what == "N":
                            c, d = arg
                            outs = u * CHUNKS - 1 if c == 1 else u * CHUNKS
                            if c == 1 and not has_prev:
                                outs = u * CHUNKS
                            pe.wait_ge(o_done.sem, o_done.after(outs - 1))
                            if not (c == 0 and d == 0):
                                pe.wait_ge(nm_copied.sem, nm_copied.after((u + d) * CHUNKS + (c - 1)))
                            nm_turn(g + d, c)
                        elif what == "O":
                            c, d = arg
                            pe.wait_ge(nm_copied.sem, nm_copied.after(
                                (u + 1) * CHUNKS if (c == 0 and has_next) else u * CHUNKS + 1))
                            pe.wait_ge(o_done.sem, o_done.after((u + d) * CHUNKS + (c - 1)))
                            o_turn(g + d, c)

                pe.wait_ge(rec_act.sem, rec_act.after(r * (2 * TILES) + (2 * TILES - 1)))
                pe.wait_ge(rec_dve.sem, rec_dve.after(r * (3 * TILES) + (3 * TILES - 1)))
                for n in range(UNITS_0):
                    unit(0, n)
                nm_turn(0, 0)
                for n in range(UNITS_0, NU):
                    unit(0, n)
                group(0, False, True)
                with pe.Fori(1, KV - 1) as g:
                    group(g, True, True)
                group(KV - 1, True, False)
                pe.wait_ge(o_done.sem, o_done.after((r * KV + KV - 1) * CHUNKS))
                o_turn(KV - 1, 1)

                def cd(i, has_c, has_d):
                    def C(k):
                        return r * TILES + i * 2 + k

                    def D(k):
                        return r * TILES + i * 2 + (k - 2)
                    if has_c:
                        for k in range(2):
                            pe.wait_ge(xc_ready.sem, xc_ready.after(C(k)))
                            turn(xc[:, k, :], psE[:, k, :], xc_turned)
                    if has_d:
                        for k in range(2):
                            pe.wait_ge(xn_ready.sem, xn_ready.after(r * (2 * TILES) + (TILES - 2) + i * 2 + k))
                            turn(xn[:, k, :], (psT if k == 0 else psO)[:], xd_turned)
                    if has_c:
                        for k in range(2):
                            pe.wait_ge(xcT_ready.sem, xcT_ready.after(C(k)))
                            pe.wait_ge(wo_added.sem, wo_added.after(C(k) - 2))
                            project(xcT[:, k], wo_s, psM[:, k, :], 0, DIM, wo_ready)
                    if has_d:
                        for k in range(2):
                            pe.wait_ge(xdT_ready.sem, xdT_ready.after(D(k)))
                            pe.wait_ge(ffn_added.sem, ffn_added.after(D(k) - 2))
                            project(xnT[:, k], wf_s, psM[:, 2 + k, :], 0, DIM, ffn_ready)

                pe.wait_ge(wo_in, r * 16 + 16)
                cd(0, True, False)
                with pe.Fori(1, PAIRS) as i:
                    cd(i, True, True)
                cd(PAIRS, False, True)

            rounds(pe, round_)

        @block.scalar
        def _(act):
            act.preload_act_table_set("natural_log_exp_and_others")
            act.wait_ge(ready, READY)
            for s in (qkv_used, rec_act, p_ready, o_copied):
                act.sem_inc(s.sem, s.credit)

            def first_rstd(q):
                act.wait_ge(var_ready.sem, var_ready.after(q))
                act.activation(ln_var[:], mv[:, :, 1], ACT.Ln, bias=eps_s[:, 0:1]).then_inc(ln_done.sem, 1)
                act.wait_ge(ln_done.sem, ln_done.after(q))
                act.activation(rs0[:], ln_var[:], ACT.Exp, scale=-0.5).then_inc(rs_ready.sem, 1)

            def copy_T(dst, src, done):
                act.activation(dst.rearrange("p a b -> p (a b)"), src, ACT.Copy).then_inc(done.sem, 1)

            def round_(b, l, r):
                def xn_T(t, k):
                    act.wait_ge(xn_turned.sem, xn_turned.after(r * TILES + t))
                    act.wait_ge(qkv_ready.sem, qkv_ready.after(r * TILES + t - 2))
                    copy_T(xnT[:, k], psE[:, k, :], xnT_ready)

                def rec_copy(t):
                    for q in (1, 3):
                        act.wait_ge(rec_turned.sem, rec_turned.after((r * TILES + t) * 5 + q))
                        act.activation(qT[:, 8 * q:8 * q + 8, t * P:(t + 1) * P],
                                       rec_banks[(t + q) % 2].rearrange("p (h n) -> p h n", h=8),
                                       ACT.Copy).then_inc(rec_act.sem, 1)

                def qkv_copy(t, k):
                    act.wait_ge(qkv_ready.sem, qkv_ready.after(r * TILES + t))
                    act.activation(qk[:, k, 0:DIM], psM[:, 2 * k, :], ACT.Copy)
                    act.activation(qk[:, k, DIM:QK], psM[:, 2 * k + 1, 0:QK - DIM], ACT.Copy).then_inc(qk_ready.sem, 1)
                    act.activation(vs[:, t, :, 0:HD], psM[:, 2 * k + 1, QK - DIM:QKV - DIM].rearrange("p (h d) -> p h d", d=HD),
                                   ACT.Copy).then_inc(qkv_used.sem, 1)

                def part_h(t, k):
                    T = r * TILES + t
                    rq = r_s[:, k, 0:DIM].rearrange("p (h a d) -> p h a d", h=HEADS, a=1)
                    rk = r_s[:, k, DIM:QK].rearrange("p (h a d) -> p h a d", h=KV, a=1)
                    act.wait_ge(rec_turned.sem, rec_turned.after((T - RECS) * 5 + 4))
                    act.wait_ge(rope_ready.sem, rope_ready.after(T))
                    act.activation(q_rec[:, t % RECS, :, 0:3, :], rq.to_broadcast([P, HEADS, 3, HD]), ACT.Copy)
                    act.activation(k_rec[:, t % RECS, :, 1:6:2, :], rk.to_broadcast([P, KV, 3, HD]), ACT.Copy).then_inc(h_ready.sem, 1)

                def part_m(t, k):
                    tq = t_s[:, k, 0:DIM].rearrange("p (h a d) -> p h a d", h=HEADS, a=1)
                    tk = t_s[:, k, DIM:QK].rearrange("p (h a d) -> p h a d", h=KV, a=1)
                    act.wait_ge(r1_ready.sem, r1_ready.after(r * TILES + t))
                    act.activation(q_rec[:, t % RECS, :, 3:5, :], tq.to_broadcast([P, HEADS, 2, HD]), ACT.Copy)
                    act.activation(k_rec[:, t % RECS, :, 2:7:2, :], tk.to_broadcast([P, KV, 3, HD]), ACT.Copy).then_inc(m_ready.sem, 1)

                first_rstd(r * (2 * PAIRS))
                xn_T(0, 0)
                for n in range(TILES + 3):
                    if n == 0:
                        first_rstd(r * (2 * PAIRS) + 1)
                    if n + 1 < TILES:
                        xn_T(n + 1, (n + 1) % 2)
                    if n >= 3:
                        rec_copy(n - 3)
                    if 0 <= n - 2 < TILES:
                        part_m(n - 2, n % 2)
                    if 0 <= n - 1 < TILES:
                        part_h(n - 1, (n - 1) % 2)
                    if n < TILES:
                        qkv_copy(n, n % 2)
                    if n % 2 == 1 and (n + 3) // 2 < PAIRS:
                        first_rstd(r * (2 * PAIRS) + (n + 3) // 2)

                def exps(g, s):
                    w = STEPS[s][3]
                    step = (r * KV + g) * NS + s
                    act.wait_ge(pv_done.sem, pv_done.after(step - PSLOTS))
                    for i, heads in enumerate(head_batches(STEPS[s])):
                        n = EXPS_BEFORE[s] + i
                        act.wait_ge(st_ready.sem, st_ready.after((r * KV + g) * NE + n))
                        act.activation(probs[:, s % PSLOTS, heads[0]:heads[0] + len(heads), 0:w],
                                       psE[:, n % 2, 0:w * len(heads)].rearrange("p (h q) -> p h q", q=w),
                                       ACT.Exp).then_inc(p_ready.sem, 1)

                def o_copy(g, c):
                    n = (r * KV + g) * CHUNKS + c
                    last_step = FIRST_1 - 1 if c == 0 else NS - 1
                    act.wait_ge(pv_done.sem, pv_done.after((r * KV + g) * NS + last_step))
                    act.wait_ge(o_turned.sem, o_turned.after(n - CHUNKS))
                    act.activation(o_T[:, c, :], psO[:], ACT.Copy).then_inc(o_copied.sem, 1)

                with act.Fori(0, KV) as g:
                    for s in range(NS):
                        exps(g, s)
                        if s == FIRST_1 + 1:
                            o_copy(g, 0)
                    o_copy(g, 1)

                def cd(i, has_c, has_d):
                    if has_c:
                        for k in range(2):
                            n = r * TILES + i * 2 + k
                            act.wait_ge(xc_turned.sem, xc_turned.after(n))
                            act.wait_ge(wo_ready.sem, wo_ready.after(n - 2))
                            copy_T(xcT[:, k], psE[:, k, :], xcT_ready)
                    if has_d:
                        for k in range(2):
                            n = r * TILES + i * 2 + (k - 2)
                            act.wait_ge(xd_turned.sem, xd_turned.after(n))
                            act.wait_ge(ffn_ready.sem, ffn_ready.after(n - 2))
                            copy_T(xnT[:, k], (psT if k == 0 else psO)[:], xdT_ready)
                    if has_c:
                        first_rstd(r * (2 * PAIRS) + PAIRS + i)

                cd(0, True, False)
                with act.Fori(1, PAIRS) as i:
                    cd(i, True, True)
                cd(PAIRS, False, True)

            rounds(act, round_)

        @block.vector
        def _(dve):
            dve.memset(eps_s[:], EPS)
            dve.memset(vs[:, :, :, HD:VW], 0.0)
            dve.memset(k_rec[:, :, :, SLOTS - 1, :], 0.0).then_inc(ready, 1)
            dve.wait_ge(ready, 1)
            dve.memset(vs[:, :, :, HD:HD + 1], 1.0)
            dve.memset(k_rec[:, :, :, SLOTS - 1, 0:3], 1.0).then_inc(ready, 1)
            dve.wait_ge(consts_in, 16 * 6)
            dve.tensor_copy(ident_b[:], ident[:])
            dve.tensor_copy(tri_b[:], rows[:, 0:P])
            dve.tensor_copy(wf_s[:], wf_raw[:]).then_inc(ready, 1)
            dve.wait_ge(ready, 3)
            dve.tensor_scalar(wf_s[:], wf_s[:], 2.0, -1.0, ALU.mult, ALU.add).then_inc(ready, 1)
            for s in (rec_ready, rec_dve, unit_used, o_done, wo_added, ffn_added):
                dve.sem_inc(s.sem, s.credit)

            def ln_link(q, n, ins):
                ins.then_inc(ln_self.sem, 1)
                wait_alone(dve, ln_self.sem, ln_self.after(q * LN_LINKS + n))

            def tile_of(i, k):
                if isinstance(i, int):
                    return xs[:, i * 2 + k, :]
                return xs[:, bass.ds(i * 2 + k, 1), :].rearrange("p a d -> p (a d)")

            def ln_stats(q, i):
                for k in range(2):
                    ins = dve.bn_stats(stats[:, k, :], tile_of(i, k))
                ln_link(q, 0, ins)
                dve.bn_aggr(mv[:, 0, :], stats[:, 0, :])
                dve.bn_aggr(mv[:, 1, :], stats[:, 1, :]).then_inc(var_ready.sem, 1)
                wait_alone(dve, var_ready.sem, var_ready.after(q))
                ln_link(q, 1, dve.tensor_scalar(var_eps[:], mv[:, :, 1], EPS, None, ALU.add))

            def ln_apply(q, i):
                dve.wait_ge(rs_ready.sem, rs_ready.after(q))
                ln_link(q, 2, dve.tensor_tensor(newton[:], rs0[:], rs0[:], ALU.mult))
                ln_link(q, 3, dve.tensor_tensor(newton2[:], newton[:], var_eps[:], ALU.mult))
                ln_link(q, 4, dve.tensor_scalar(newton[:], newton2[:], -0.5, 1.5, ALU.mult, ALU.add))
                ln_link(q, 5, dve.tensor_tensor(rstd[:], rs0[:], newton[:], ALU.mult))
                for k in range(2):
                    dve.tensor_scalar(xn[:, k, :], tile_of(i, k), mv[:, k, 0:1], rstd[:, k:k + 1],
                                      ALU.subtract, ALU.mult).then_inc(xn_ready.sem, 1)

            def round_(b, l, r):
                def ln_a_stats(i):
                    dve.wait_ge(x_in[i], b * 16 + 16)
                    wait_alone(dve, ffn_added.sem, ffn_added.after(r * TILES - TILES + i * 2 + 1))
                    ln_stats(r * (2 * PAIRS) + i, i)

                def ln_a(i):
                    wait_alone(dve, xn_turned.sem, xn_turned.after(r * TILES + i * 2 - 1))
                    ln_apply(r * (2 * PAIRS) + i, i)

                def rec_copy(t):
                    for q in (0, 2, 4):
                        dve.wait_ge(rec_turned.sem, rec_turned.after((r * TILES + t) * 5 + q))
                        to = qT[:, 8 * q:8 * q + 8, t * P:(t + 1) * P] if q < 4 else kT[:, :, t * P:(t + 1) * P]
                        dve.tensor_copy(to, rec_banks[(t + q) % 2].rearrange("p (h n) -> p h n", h=8)).then_inc(rec_dve.sem, 1)

                def rope(t, k):
                    T = r * TILES + t
                    dve.wait_ge(qk_ready.sem, qk_ready.after(T))
                    c = cos_s[:, bass.ds(l, 1), t, :]
                    dve.tensor_tensor(r_s[:, k].rearrange("p (h d) -> p h d", d=HD),
                                      qk[:, k].rearrange("p (h d) -> p h d", d=HD),
                                      c.to_broadcast([P, HEADS + KV, HD]), ALU.mult).then_inc(cos_self.sem, 1)
                    dve.wait_ge(cos_self.sem, cos_self.after(T))
                    dve.wait_ge(sin_ready.sem, sin_ready.after(T))
                    dve.tensor_tensor(r_s[:, k], r_s[:, k], t_s[:, k], ALU.add).then_inc(rope_ready.sem, 1)

                def part_l(t, k):
                    dve.wait_ge(m_ready.sem, m_ready.after(r * TILES + t))
                    tq = t_s[:, k, 0:DIM].rearrange("p (h a d) -> p h a d", h=HEADS, a=1)
                    tk = t_s[:, k, DIM:QK].rearrange("p (h d) -> p h d", h=KV)
                    dve.tensor_tensor(q_rec[:, t % RECS, :, 5:7, :], tq.to_broadcast([P, HEADS, 2, HD]),
                                      q_rec[:, t % RECS, :, 3:5, :], ALU.subtract)
                    dve.tensor_tensor(k_rec[:, t % RECS, :, 0, :], tk, k_rec[:, t % RECS, :, 2, :], ALU.subtract).then_inc(rec_ready.sem, 1)

                ln_a_stats(0)
                ln_a(0)
                ln_a_stats(1)
                for n in range(TILES + 3):
                    if n >= 3:
                        rec_copy(n - 3)
                    if n % 2 == 0 and n // 2 + 1 < PAIRS:
                        ln_a(n // 2 + 1)
                    if 0 <= n - 1 < TILES:
                        rope(n - 1, (n - 1) % 2)
                    if 0 <= n - 2 < TILES:
                        part_l(n - 2, n % 2)
                    if n % 2 == 1 and (n + 3) // 2 < PAIRS:
                        ln_a_stats((n + 3) // 2)

                def unit(g, n):
                    M = (r * KV + g) * NU + n
                    qt, heads = UNITS[n]
                    keys = (qt + 1) * P
                    if n in (0, UNITS_0):
                        dve.wait_ge(nm_split.sem, nm_split.after((r * KV + g - 1) * CHUNKS + (0 if n == 0 else 1)))
                    dve.wait_ge(unit_ready.sem, unit_ready.after(M))
                    banks = psM[:, 2 * (n % 2):2 * (n % 2) + 2, :].rearrange("p a b -> p (a b)")
                    pitch = keys if keys != 384 else 512
                    src = banks[:, 0:pitch * len(heads)].rearrange("p (h k) -> p h k", k=pitch)[:, :, 0:keys]
                    dve.tensor_reduce(mx[:, qt, heads[0]:heads[0] + len(heads)], src, AX.X, ALU.max).then_inc(unit_used.sem, 1)

                def nm_copy(g, c):
                    u = r * KV + g
                    dve.wait_ge(nm_turned.sem, nm_turned.after(u * CHUNKS + c))
                    dve.wait_ge(nm_in[c], u * 16 + 16)
                    dve.tensor_copy(nm_rows[:, c, :], nm_ps[0:3 * REP, 0:QCHUNK]).then_inc(nm_copied.sem, 1)

                def o_divide(g, c):
                    n = (r * KV + g) * CHUNKS + c
                    dve.wait_ge(o_turned.sem, o_turned.after(n))
                    o = psT[:].rearrange("p (t h d) -> p t h d", t=QT_PER_CHUNK, h=REP)
                    dve.reciprocal(den[:], o[:, :, :, HD]).then_inc(o_self.sem, 1)
                    dve.wait_ge(o_self.sem, o_self.after(n))
                    to = attn[:, c * QT_PER_CHUNK:(c + 1) * QT_PER_CHUNK, bass.ds(g * (REP * HD), REP * HD)]
                    dve.tensor_tensor(to.rearrange("p t (h d) -> p t h d", h=REP), o[:, :, :, 0:HD],
                                      den[:].rearrange("p t (h a) -> p t h a", a=1).to_broadcast([P, QT_PER_CHUNK, REP, HD]),
                                      ALU.mult).then_inc(o_done.sem, 1)

                def group(g, has_prev, has_next):
                    for what, *arg in group_order(has_prev, has_next):
                        if what == "U":
                            unit(g + 1, arg[0])
                        elif what == "N":
                            nm_copy(g + arg[1], arg[0])
                        elif what == "O":
                            o_divide(g + arg[1], arg[0])

                for n in range(UNITS_0):
                    unit(0, n)
                nm_copy(0, 0)
                for n in range(UNITS_0, NU):
                    unit(0, n)
                group(0, False, True)
                with dve.Fori(1, KV - 1) as g:
                    group(g, True, True)
                group(KV - 1, True, False)
                o_divide(KV - 1, 1)

                def add_wo(i, k):
                    n = r * TILES + i * 2 + k
                    dve.wait_ge(wo_ready.sem, wo_ready.after(n))
                    xt = xs[:, bass.ds(i * 2 + k, 1), :].rearrange("p a d -> p (a d)")
                    dve.tensor_tensor(xt, psM[:, k, :], xt, ALU.add).then_inc(wo_added.sem, 1)

                def add_ffn(i, k):
                    n = r * TILES + i * 2 + (k - 2)
                    dve.wait_ge(ffn_ready.sem, ffn_ready.after(n))
                    xt = xs[:, bass.ds(i * 2 + (k - 2), 1), :].rearrange("p a d -> p (a d)")
                    dve.scalar_tensor_tensor(out=xt, in0=psM[:, 2 + k, :], scalar=scale_s[:, 0:1], in1=xt,
                                             op0=ALU.mult, op1=ALU.add).then_inc(ffn_added.sem, 1)

                def cd(i, has_c, has_d):
                    if has_c:
                        for k in range(2):
                            add_wo(i, k)
                        wait_alone(dve, wo_added.sem, wo_added.after(r * TILES + i * 2 + 1))
                        ln_stats(r * (2 * PAIRS) + PAIRS + i, i)
                        wait_alone(dve, xd_turned.sem, xd_turned.after(r * TILES + i * 2 - 1))
                        ln_apply(r * (2 * PAIRS) + PAIRS + i, i)
                    if has_d:
                        for k in range(2):
                            add_ffn(i, k)

                cd(0, True, False)
                with dve.Fori(1, PAIRS) as i:
                    cd(i, True, True)
                cd(PAIRS, False, True)

            rounds(dve, round_)

        @block.gpsimd
        def _(pool):
            pool.wait_ge(ready, READY)
            pool.sem_inc(nm_split.sem, nm_split.credit)

            def round_(b, l, r):
                def rope_sin(t, k):
                    T = r * TILES + t
                    wait_alone(pool, qk_ready.sem, qk_ready.after(T))
                    wait_alone(pool, rec_ready.sem, rec_ready.after(T - 2))
                    x4 = qk[:, k].rearrange("p (h a d) -> p h a d", a=2, d=HALF)
                    t4 = t_s[:, k].rearrange("p (h a d) -> p h a d", a=2, d=HALF)
                    sn = sin_s[:, bass.ds(l, 1), t, :]
                    for a in range(2):
                        ins = pool.tensor_tensor(t4[:, :, a, :], x4[:, :, 1 - a, :],
                                                 sn[:, :, a * HALF:(a + 1) * HALF].to_broadcast([P, HEADS + KV, HALF]), ALU.mult)
                    ins.then_inc(sin_ready.sem, 1)

                def rest(t, k):
                    wait_alone(pool, h_ready.sem, h_ready.after(r * TILES + t))
                    rq = r_s[:, k, 0:DIM].rearrange("p (h d) -> p h d", d=HD)
                    rk = r_s[:, k, DIM:QK].rearrange("p (h d) -> p h d", d=HD)
                    tq = t_s[:, k, 0:DIM].rearrange("p (h d) -> p h d", d=HD)
                    tk = t_s[:, k, DIM:QK].rearrange("p (h d) -> p h d", d=HD)
                    pool.tensor_tensor(tq, rq, q_rec[:, t % RECS, :, 0, :], ALU.subtract)
                    pool.tensor_tensor(tk, rk, k_rec[:, t % RECS, :, 1, :], ALU.subtract).then_inc(r1_ready.sem, 1)

                pool.memset(q_rec_last, 0.0)
                for n in range(1, TILES + 2):
                    if 0 <= n - 2 < TILES:
                        rest(n - 2, n % 2)
                    if n - 1 < TILES:
                        rope_sin(n - 1, (n - 1) % 2)

                def nm_parts_of(g, c):
                    n = (r * KV + g) * CHUNKS + c
                    links = [0]

                    def link(ins):
                        ins.then_inc(nm_self.sem, 1)
                        wait_alone(pool, nm_self.sem, nm_self.after(n * NM_LINKS + links[0]))
                        links[0] += 1

                    last_unit = UNITS_0 - 1 if c == 0 else NU - 1
                    wait_alone(pool, unit_used.sem, unit_used.after((r * KV + g) * NU + last_unit))
                    wait_alone(pool, nm_turned.sem, nm_turned.after(n - 2))
                    link(pool.tensor_scalar(nm[:], mx[:, c * QT_PER_CHUNK:(c + 1) * QT_PER_CHUNK, :], -1.0, None, ALU.mult))
                    link(pool.tensor_copy(nm_parts[:, c, :, 0, :], nm[:]))
                    link(pool.tensor_tensor(nm_r[:], nm[:], nm_parts[:, c, :, 0, :], ALU.subtract))
                    link(pool.tensor_copy(nm_parts[:, c, :, 1, :], nm_r[:]))
                    pool.tensor_tensor(nm_parts[:, c, :, 2, :], nm_r[:], nm_parts[:, c, :, 1, :], ALU.subtract).then_inc(nm_split.sem, 1)
                    assert links[0] == NM_LINKS

                def mask(g, s):
                    u = r * KV + g
                    wait_alone(pool, p_ready.sem, p_ready.after(u * NE + last_exp(s)))
                    d = probs[:, s % PSLOTS, :, 0:P]
                    pool.affine_select(out=d, in_=d, compare_op=ALU.is_ge, fill=0.0, base=0,
                                       pattern=[[0, REP], [1, P]], channel_multiplier=-1).then_inc(masked.sem, 1)

                def group(g, has_next):
                    u = r * KV + g
                    wait_alone(pool, pv_done.sem, pv_done.after(u * NS - 1))
                    pool.tensor_copy(v_grp[:], vs[:, :, bass.ds(g, 1), :].rearrange("p t a d -> p t (a d)")).then_inc(v_ready.sem, 1)
                    for s in DIAGONAL:
                        mask(g, s)
                        if has_next and s == SPLIT_AFTER:
                            nm_parts_of(g + 1, 0)
                    if has_next:
                        nm_parts_of(g + 1, 1)

                nm_parts_of(0, 0)
                nm_parts_of(0, 1)
                with pool.Fori(0, KV - 1) as g:
                    group(g, True)
                group(KV - 1, False)

                def tile_out(t, k):
                    n = r * TILES + t
                    wait_alone(pool, xc_turned.sem, xc_turned.after(n - 2))
                    pool.tensor_copy(xc[:, k, :], attn[:, bass.ds(t, 1), :].rearrange("p a d -> p (a d)")).then_inc(xc_ready.sem, 1)

                wait_alone(pool, o_done.sem, o_done.after((r * KV + KV - 1) * CHUNKS + 1))
                with pool.Fori(0, PAIRS) as i:
                    tile_out(i * 2, 0)
                    tile_out(i * 2 + 1, 1)

            rounds(pool, round_)


def tables():
    import numpy as np
    cos, sin = [], []
    for base in (10000.0, 500000.0):
        inv = (np.float32(1.0) / np.power(np.float32(base), np.arange(0, HD, 2, dtype=np.float32) / np.float32(HD))).astype(np.float32)
        ang = (np.arange(SEQ, dtype=np.float32)[:, None] * inv[None, :]).astype(np.float64)
        c, s = 0.5 * np.cos(ang), 0.5 * np.sin(ang)
        cos.append(np.concatenate([c, c], 1))
        sin.append(np.concatenate([-s, s], 1))
    shape = lambda a: np.ascontiguousarray(np.stack(a).astype(np.float32).reshape(LAYERS, TILES, P, HD).transpose(2, 0, 1, 3))
    return shape(cos), shape(sin)


def kernel(L0_attn_a_x, L0_attn_a_w_qkv, L0_attn_a_w_o, L0_attn_b_w_qkv, L0_attn_b_w_o, L0_ffn_kernel, L0_ffn_scale):
    import numpy as np
    import concourse.bacc as bacc
    from concourse.bass_utils import run_bass_kernel_spmd

    wa = np.asarray(L0_attn_a_w_qkv)
    wa_qk = wa[:, :QK].reshape(DIM, QK // HD, HALF, 2).transpose(0, 1, 3, 2).reshape(DIM, QK)
    wa = np.concatenate([wa_qk, wa[:, QK:]], 1)
    wb = np.asarray(L0_attn_b_w_qkv).T
    cos, sin = tables()
    tri = np.where(np.arange(P)[None, :] > np.arange(P)[:, None], np.float32(-1e30), np.float32(0)).astype(np.float32)
    arrays = {
        "x": np.ascontiguousarray(L0_attn_a_x),
        "w_qkv": np.ascontiguousarray(np.stack([wa, wb])),
        "w_o": np.ascontiguousarray(np.stack([np.asarray(L0_attn_a_w_o), np.asarray(L0_attn_b_w_o).T])),
        "w_ffn": np.ascontiguousarray(L0_ffn_kernel),
        "scale": np.ascontiguousarray(np.asarray(L0_ffn_scale).reshape(1)),
        "cos": cos,
        "sin": sin,
        "eye": np.eye(P, dtype=np.float32),
        "tri": tri,
    }
    nc = bacc.Bacc("TRN2", target_bir_lowering=False, num_devices=1)
    args = [nc.dram_tensor(f"in_{n}", a.shape, mybir.dt.from_np(a.dtype), kind="ExternalInput").ap() for n, a in arrays.items()]
    out = nc.dram_tensor("out_x", (BATCH, SEQ, DIM), F32, kind="ExternalOutput").ap()
    build(nc, *args, out)
    res = run_bass_kernel_spmd(nc, [{f"in_{n}": a for n, a in arrays.items()}], core_ids=[0])
    return res.results[0]["out_x"]
```

```python
from contextlib import ExitStack

import concourse.bass as bass
from concourse import mybir

ALU = mybir.AluOpType
ACT = mybir.ActivationFunctionType
AX = mybir.AxisListType
F32 = mybir.dt.float32
BF16 = mybir.dt.bfloat16
F32R = mybir.dt.float32r
U8 = mybir.dt.uint8

P = 128
SEQ = 1024
DIM = 512
HEADS = 32
KV = 8
REP = HEADS // KV
HD = DIM // HEADS
HALF = HD // 2
BATCH = 2
LAYERS = 2
EPS = 1e-5

TILES = SEQ // P
PAIRS = TILES // 2
KC = DIM // P
QKV = DIM + 2 * KV * HD
QK = DIM + KV * HD
QCHUNK = 512
CHUNKS = SEQ // QCHUNK
QT_PER_CHUNK = QCHUNK // P
VW = 32
PSLOTS = 3

SLOTS = 8
MAXROW = (SLOTS - 1) * HD
DEPTH = MAXROW + 3
RECS = 3

AHEAD = TILES // 2


def words(text):
    return [(w.split(".")[0], *(int(a) for a in w.split(".")[1:])) for w in text.split()]


CD_TILES = words("C.0 C.1 C.2 C.3 D.0 D.1 C.4 C.5 C.6 C.7 D.2 D.3 D.4 D.5 D.6 D.7")
TURNS = TILES + len(CD_TILES)


def c_turn(t):
    return TILES + CD_TILES.index(("C", t))


def d_turn(t):
    return TILES + CD_TILES.index(("D", t))


assert all(X % 2 == t % 2 for X, (what, t) in enumerate(CD_TILES)) and CD_TILES[-1] == ("D", TILES - 1)


class Signal:

    def __init__(self, sem, credit=0):
        self.sem, self.credit = sem, credit

    def after(self, n):
        return n + (self.credit + 1)


def score_steps():
    out = []
    for c in range(CHUNKS):
        before = list(range(c * QT_PER_CHUNK))
        diagonal = list(range(c * QT_PER_CHUNK, (c + 1) * QT_PER_CHUNK))
        order = [kb for pair in zip(before, diagonal) for kb in pair] if before else diagonal
        for kb in order:
            q0 = max(c * QCHUNK, kb * P)
            out.append((c, kb, q0, (c + 1) * QCHUNK - q0))
    return out


def head_batches(step):
    per = max(1, QCHUNK // step[3])
    return [list(range(h, min(REP, h + per))) for h in range(0, REP, per)]


def last_exp(s):
    return EXPS_BEFORE[s] + len(head_batches(STEPS[s])) - 1


def max_units():
    out = []
    for qt in range(TILES):
        keys = (qt + 1) * P
        per = max(1, 2 * (QCHUNK // keys)) if keys <= QCHUNK else 1
        per = min(per, REP)
        out += [(qt, list(range(h, h + per))) for h in range(0, REP, per)]
    return out


STEPS = score_steps()
UNITS = max_units()
NS = len(STEPS)
NU = len(UNITS)
ND = TILES
UNITS_0 = sum(1 for qt, _ in UNITS if qt < QT_PER_CHUNK)
DIAGONAL = [s for s, (c, kb, q0, w) in enumerate(STEPS) if kb >= c * QT_PER_CHUNK]
SPLIT_AFTER = 5
WO_HI_AFTER = [3, 4, 5, 6]
WO_LO_AFTER = [5, 7, 9, 11]
FIRST_1 = QT_PER_CHUNK
EXPS_BEFORE = [sum(len(head_batches(t)) for t in STEPS[:s]) for s in range(NS)]
NE = sum(len(head_batches(t)) for t in STEPS)
assert NE % 2 == 0 and NS % PSLOTS == 0 and NU % 2 == 0


GROUP_ORDER = """
S.0.0 S.0.1 U.0 U.1 S.0.2 S.0.3 U.2
S.1.0 N.1.0 S.1.1 U.3 S.1.2 U.4 S.1.3 PV.0
S.2.0 U.5 S.2.1 U.6
S.3.0 PV.1
S.4.0 O.1.-1 S.4.1 U.7 S.4.2 U.8 S.4.3 PV.2
S.5.0 U.9 S.5.1 U.10 S.5.2 PV.3 S.5.3 U.11
S.6.0 U.12 S.6.1 PV.4 S.6.2 S.6.3 U.13 N.0.1 U.14
S.7.0 S.7.1 PV.5 S.7.2 S.7.3 U.15 U.16
S.8.0 S.8.1 PV.6 S.8.2 S.8.3 U.17 U.18
S.9.0 S.9.1 PV.7
S.10.0 PV.8 S.10.1 S.10.2 U.19 U.20 S.10.3
S.11.0 PV.9 O.0.0 U.21 PV.10 PV.11
"""


LAST_ORDER = """
S.0.0 S.0.1 S.0.2 S.0.3
S.1.0 S.1.1 N.1.0 S.1.2 PV.0 S.1.3
S.2.0 O.1.-1 S.2.1
S.3.0 PV.1
S.4.0 PV.2 S.4.1 PV.3 S.4.2 S.4.3
S.5.0 S.5.1 O.0.0 PV.4 S.5.2 S.5.3 CT.0
S.6.0 CT.1 S.6.1 PV.5 S.6.2 CP.0 S.6.3
S.7.0 CT.2 S.7.1 CP.1 LS.0 S.7.2 PV.6 S.7.3
S.8.0 CT.3 S.8.1 CP.2 LR.0 S.8.2 LM.0 LN.0 PV.7 S.8.3
S.9.0 CP.3 LS.1 S.9.1 DT.0 PV.8
S.10.0 S.10.1 DT.1 PV.9 S.10.2 S.10.3 LR.1
S.11.0 LM.1 LN.1 PV.10 PV.11
"""
TAIL_ORDER = """
DP.0 O.1.0 DP.1 CT.4 CT.5 CP.4 CT.6 WQ.0 CP.5 LS.2 CT.7 LR.2 WQ.1 T.2 CP.6 LM.2 T.3 LN.2 H.2
WQ.2 CP.7 H.3 LS.3 WQ.3 LR.3 T.4 DP.2 LM.3 T.5 H.4 LN.3 DP.3 H.5 LS.4 DP.4 T.6 H.6 LR.4 DP.5
LM.4 T.7 LN.4 H.7 DP.6 TA.0 DP.7
"""


def units_of(qt):
    return [n for n, (q, heads) in enumerate(UNITS) if q == qt]


LAG = {"TX": -1, "Q": 0, "R": 3, "U": 4, "HI": -1, "LO": -1, "QC": 0, "COS": 1, "ROPE": 1, "PH": 1, "PM": 2, "PL": 2,
       "RC": 3, "ST": -4, "RS": -3, "AP": -2}
PE_SLOT = "R.0 TX U.0 R.1 Q.0 U.1 R.2 U.2 R.3 Q.1 Q.2 R.4 U.3 Q.3"
ACT_SLOT = "HI RC.1 PM RC.2 RS RC.3 PH QC"
DVE_SLOT = "AP RC.0 U.0 COS LO U.1 ROPE U.2 PL RC.4 ST U.3"
SLOTS_A = range(-4, TILES + 4)
SLOT_NM = TILES + 2


def slot_work(text, n):
    out = []
    for what, *arg in words(text):
        t = n - LAG[what]
        if what in ("ST", "RS", "AP"):
            if t % 2 == 0 and 1 <= t // 2 < PAIRS:
                out.append((what, arg, t // 2))
        elif 0 <= t < TILES and (what != "U" or arg[0] < len(units_of(t))):
            out.append((what, arg, t))
    return out


def qkv_bank(t):
    return 2 if t == 1 else 0


def unit_pair(g_is_first, n):
    return n % 2 if not g_is_first or UNITS[n][0] > QT_PER_CHUNK else 1


def group_order(has_prev, has_next):
    if not has_next:
        return words(LAST_ORDER)
    return [w for w in words(GROUP_ORDER) if has_prev or w[0] != "O" or w[2] == 0]


READY = 3
LS_LINKS, LM_LINKS = 2, 4
NM_LINKS = 4


def build(nc, x, w_qkv, w_o, w_ffn, scale, cos, sin, eye, tri, out):
    with ExitStack() as ctx:
        def sb(name, shape, dt=F32):
            return ctx.enter_context(nc.sbuf_tensor(name, shape, dt))

        def ps(name, shape, dt=F32):
            return ctx.enter_context(nc.psum_tensor(name, shape, dt))

        def sem(name):
            return ctx.enter_context(nc.semaphore(name))

        xs = sb("xs", [P, TILES, DIM])
        wq_hi = sb("wq_hi", [P, KC, QKV], F32R)
        w_lo = sb("w_lo", [P, KC, QKV], F32R)
        wo_hi = sb("wo_hi", [P, KC, DIM], F32R)
        wf_s = sb("wf_s", [P, KC, DIM], F32R)
        cos_s = sb("cos_s", [P, LAYERS, TILES, HD])
        sin_s = sb("sin_s", [P, LAYERS, TILES, HD])
        ident = sb("ident", [P, P])
        ident_b = sb("ident_b", [P, P], BF16)
        tri_b = sb("tri_b", [P, P], BF16)
        scale_s = sb("scale_s", [P, 1])
        eps_s = sb("eps_s", [P, 1])

        stats = sb("stats", [P, 2, 2, 6])
        mv = sb("mv", [P, 2, 2, 2])
        var_eps = sb("var_eps", [P, 2, 2])
        ln_var = sb("ln_var", [P, 2, 2])
        rs0 = sb("rs0", [P, 2, 2])
        newton = sb("newton", [P, 2])
        newton2 = sb("newton2", [P, 2])
        rstd = sb("rstd", [P, 2, 2])
        xn = sb("xn", [P, 2, DIM])
        xT_hi = sb("xT_hi", [P, 2, KC, P], F32R)
        xT_lo = sb("xT_lo", [P, 2, KC, P], F32R)

        qT = sb("qT", [P, HEADS, SEQ], BF16)
        kT = sb("kT", [P, KV, SEQ], BF16)
        vs = sb("vs", [P, TILES, KV, HD])
        v_grp = sb("v_grp", [P, TILES, VW])
        k_rec = sb("k_rec", [P, RECS, KV, SLOTS, HD], BF16)
        o_T = k_rec[:].rearrange("p a h s d -> p (a h s d)").bitcast(F32)[:, 0:CHUNKS * QCHUNK].rearrange(
            "p (c q) -> p c q", c=CHUNKS)
        mx = sb("mx", [P, TILES, REP])
        nm = sb("nm", [P, QT_PER_CHUNK, REP])
        nm_r = sb("nm_r", [P, QT_PER_CHUNK, REP])
        nm_parts = sb("nm_parts", [P, CHUNKS, QT_PER_CHUNK, 3, REP], BF16)
        nm_rows = sb("nm_rows", [3 * REP, CHUNKS, QCHUNK], BF16)
        den = sb("den", [P, QT_PER_CHUNK, REP])

        attn = sb("attn", [P, TILES, DIM])
        rows = attn[:].rearrange("p t d -> p (t d)")
        qk = rows[:, 0:2 * QK].rearrange("p (b n) -> p b n", b=2)
        r_s = rows[:, 2 * QK:4 * QK].rearrange("p (b n) -> p b n", b=2)
        t_s = rows[:, 4 * QK:6 * QK].rearrange("p (b n) -> p b n", b=2)
        probs = sb("probs", [P, PSLOTS, REP, QCHUNK])
        q_rec = probs[:].rearrange("p a b c -> p (a b c)").bitcast(BF16).rearrange(
            "p (b h s d) -> p b h s d", b=RECS, h=HEADS, s=SLOTS)
        q_rec_last = probs[:].rearrange("p a b c -> p (a b c)").rearrange(
            "p (r n) -> p r n", n=SLOTS * HD // 2)[:, :, MAXROW // 2:]
        probs_flat = probs[:].rearrange("p a b c -> p (a b c)")
        wq_raw = probs_flat[:, 0:KC * QKV].rearrange("p (c n) -> p c n", c=KC)
        wf_raw = probs_flat[:, KC * QKV:KC * QKV + KC * DIM // 4].bitcast(U8).rearrange("p (c n) -> p c n", c=KC)
        wo_raw = attn[:, TILES - KC:TILES, :]

        psM = ps("psM", [P, 4, 512])
        psE = ps("psE", [P, 2, 512])
        psO = ps("psO", [P, 512])
        psT = ps("psT", [P, 512])
        rec_banks = [psT[:].bitcast(BF16), psO[:].bitcast(BF16)]
        nm_ps = psT[:].bitcast(BF16)
        nm_ps_0 = psE[:, 0, :].bitcast(BF16)

        consts_in = sem("consts_in")
        eye_in = sem("eye_in")
        ready = sem("ready")
        x_in = [sem(f"x_in{i}") for i in range(PAIRS)]
        x_out = [sem(f"x_out{i}") for i in range(PAIRS)]
        wq_in, wo_in = sem("wq_in"), sem("wo_in")
        wq_hi_done, wo_hi_done = sem("wq_hi_done"), sem("wo_hi_done")
        wq_lo_done, wo_lo_done = sem("wq_lo_done"), sem("wo_lo_done")
        ls_self, lm_self = Signal(sem("ls_self")), Signal(sem("lm_self"))
        var_ready = Signal(sem("var_ready"))
        ln_done = Signal(sem("ln_done"))
        rs_ready = Signal(sem("rs_ready"))
        xn_ready = Signal(sem("xn_ready"), 96)
        turned = Signal(sem("turned"), 2)
        hi_ready = Signal(sem("hi_ready"), 2)
        lo_ready = Signal(sem("lo_ready"), 2)
        projected = Signal(sem("projected"), 2)
        qk_ready = Signal(sem("qk_ready"))
        qkv_used = Signal(sem("qkv_used"), 2)
        sin_ready = Signal(sem("sin_ready"))
        cos_self = Signal(sem("cos_self"))
        rope_ready = Signal(sem("rope_ready"))
        h_ready = Signal(sem("h_ready"))
        r1_ready = Signal(sem("r1_ready"))
        m_ready = Signal(sem("m_ready"))
        rec_ready = Signal(sem("rec_ready"), 2)
        rec_turned = Signal(sem("rec_turned"), 5 * RECS)
        rec_dve = Signal(sem("rec_dve"), 64)
        rec_act = Signal(sem("rec_act"), 32)
        unit_ready = Signal(sem("unit_ready"))
        unit_used = Signal(sem("unit_used"), 2)
        nm_split = Signal(sem("nm_split"), 2)
        nm_self = Signal(sem("nm_self"))
        nm_turned = Signal(sem("nm_turned"), 2)
        nm_copied = Signal(sem("nm_copied"))
        nm_in = [sem(f"nm_in{c}") for c in range(CHUNKS)]
        st_ready = Signal(sem("st_ready"))
        p_ready = Signal(sem("p_ready"), 2)
        masked = Signal(sem("masked"))
        v_ready = Signal(sem("v_ready"))
        pv_done = Signal(sem("pv_done"), NS)
        o_copied = Signal(sem("o_copied"), 2)
        o_turned = Signal(sem("o_turned"), 2)
        o_self = Signal(sem("o_self"))
        o_done = Signal(sem("o_done"), 2)
        wo_added = Signal(sem("wo_added"), 16)
        ffn_added = Signal(sem("ffn_added"), 32)

        block = ctx.enter_context(nc.Block())

        passed = sem("passed")

        def wait_alone(eng, signal, value):
            eng.wait_ge(signal, value)
            eng.sem_inc(passed, 1)

        def rounds(eng, body):
            with eng.Fori(0, BATCH) as b:
                with eng.Fori(0, LAYERS) as l:
                    body(b, l, b * LAYERS + l)

        @block.sync
        def _(sp):
            for s in (*x_out, *nm_in):
                sp.sem_inc(s, 16)

            def load_pair(b, i):
                src = x[b].rearrange("(t p) d -> p t d", p=P)[:, 2 * i:2 * i + 2, :]
                sp.dma_start(xs[:, 2 * i:2 * i + 2, :], src).then_inc(x_in[i], 16)

            def load_wq(l):
                sp.dma_start(wq_raw, w_qkv[l].rearrange("(c p) n -> p c n", p=P)).then_inc(wq_in, 16)

            def load_consts():
                wv = w_ffn.rearrange("(c p) n -> p c n", p=P)
                sp.dma_start(wf_raw[:], wv).then_inc(consts_in, 16)
                sp.dma_start(cos_s[:], cos).then_inc(consts_in, 16)
                sp.dma_start(sin_s[:], sin).then_inc(consts_in, 16)
                sp.dma_start(scale_s[:], scale.rearrange("(a b) -> a b", a=1).to_broadcast([P, 1])).then_inc(consts_in, 16)
                sp.dma_start(rows[:, 0:P], tri).then_inc(consts_in, 16)

            def put_nm(r, g, c):
                sp.wait_ge(nm_copied.sem, nm_copied.after((r * KV + g) * CHUNKS + c))
                sp.dma_start(
                    qT[MAXROW:MAXROW + 3, bass.ds(g * REP, REP), c * QCHUNK:(c + 1) * QCHUNK],
                    nm_rows[:, c, :],
                ).then_inc(nm_in[c], 16)

            def layers(b):
                with sp.Fori(0, LAYERS) as l:
                    r = b * LAYERS + l
                    put_nm(r, 0, 0)
                    wait_alone(sp, rec_ready.sem, rec_ready.after(r * TILES + (TILES - 1)))
                    sp.dma_start(wo_raw, w_o[l].rearrange("(c p) n -> p c n", p=P)).then_inc(wo_in, 16)
                    put_nm(r, 0, 1)
                    with sp.Fori(1, KV) as g:
                        for c in range(CHUNKS):
                            put_nm(r, g, c)
                    wait_alone(sp, pv_done.sem, pv_done.after(r * (KV * NS) + (KV * NS - 1)))
                    load_wq((LAYERS - 1) - l)

            def store_pair(b, i):
                sp.wait_ge(ffn_added.sem, ffn_added.after(b * (LAYERS * TILES) + ((LAYERS - 1) * TILES + 2 * i + 1)))
                dst = out[b].rearrange("(t p) d -> p t d", p=P)[:, 2 * i:2 * i + 2, :]
                sp.dma_start(dst, xs[:, 2 * i:2 * i + 2, :]).then_inc(x_out[i], 16)

            load_pair(0, 0)
            sp.dma_start(ident[:], eye).then_inc(eye_in, 16)
            load_wq(0)
            load_consts()
            for i in range(1, PAIRS):
                load_pair(0, i)
            with sp.Fori(0, BATCH - 1) as b:
                layers(b)
                for i in range(PAIRS):
                    store_pair(b, i)
                    wait_alone(sp, x_out[i], b * 16 + 32)
                    load_pair(b + 1, i)
            layers(BATCH - 1)
            sp.sem_inc(x_in[0], 16)
            for i in range(PAIRS):
                store_pair(BATCH - 1, i)
            for i in range(PAIRS):
                sp.wait_ge(x_out[i], 16 * BATCH + 16)

        @block.tensor
        def _(pe):
            for s in (nm_turned, turned, projected, rec_turned, pv_done, o_turned):
                pe.sem_inc(s.sem, s.credit)

            def turn(src, dst, done):
                for c in range(KC):
                    ins = pe.transpose(dst[:, c * P:(c + 1) * P], src[:, c * P:(c + 1) * P], ident[:])
                ins.then_inc(done.sem, 1)

            def turn_xn(r, t, k):
                pe.wait_ge(xn_ready.sem, xn_ready.after(r * (2 * TILES) + t))
                pe.wait_ge(lo_ready.sem, lo_ready.after(r * TURNS + (t - 2)))
                turn(xn[:, k, :], psE[:, k, :], turned)

            def products(his, los, n0, n1):
                return [(xT_hi, w, c, n0, n1) for w in (his, los) if w is not None for c in range(KC)] + [
                    (xT_lo, his, c, n0, n1) for c in range(KC)]

            def multiply(k, dst, some, first, last):
                for i, (xT, w, c, n0, n1) in enumerate(some):
                    ins = pe.matmul(dst, xT[:, k, c, :], w[:, c, n0:n1], start=first and i == 0,
                                    stop=last and i == len(some) - 1)
                return ins

            def round_(b, l, r):
                def wait_hi(X):
                    pe.wait_ge(hi_ready.sem, hi_ready.after(r * TURNS + X))

                def wait_lo(X):
                    pe.wait_ge(lo_ready.sem, lo_ready.after(r * TURNS + X))

                def qkv(t, k, part):
                    T = r * TILES + t
                    if part == 0:
                        wait_hi(t)
                        pe.wait_ge(qkv_used.sem, qkv_used.after(T - 2 if t in (1, 2) else T - 1))
                        if t == 1:
                            pe.wait_ge(ffn_added.sem, ffn_added.after(T - 2))
                        if t == 0:
                            pe.wait_ge(wq_hi_done, r * KC + KC)
                    if part == 1 and t == 0:
                        pe.wait_ge(wq_lo_done, r * KC + KC)
                    if part == 2:
                        wait_lo(t)
                    if part < 3:
                        some = products(wq_hi, w_lo, 0, DIM)[part * KC:(part + 1) * KC]
                        multiply(k, psM[:, qkv_bank(t), :], some, part == 0, part == 2)
                    else:
                        some = products(wq_hi, w_lo, DIM, QKV)
                        multiply(k, psM[:, qkv_bank(t) + 1, 0:QKV - DIM], some, True, True).then_inc(projected.sem, 1)

                def turn_rec(t, q):
                    T = r * TILES + t
                    if q == 0:
                        if t == 0:
                            pe.wait_ge(ready, READY)
                        pe.wait_ge(rec_ready.sem, rec_ready.after(T))
                    if q in (0, 3, 4):
                        pe.wait_ge(rec_act.sem, rec_act.after(T * 3 + {0: -1, 3: 0, 4: 1}[q]))
                    else:
                        pe.wait_ge(rec_dve.sem, rec_dve.after(T * 2 + {1: -1, 2: 0}[q]))
                    bank = rec_banks[(t + q) % 2]
                    for h in range(8):
                        src = q_rec[:, t % RECS, 8 * q + h] if q < 4 else k_rec[:, t % RECS, h]
                        ins = pe.transpose(bank[:, h * P:(h + 1) * P], src.rearrange("p s d -> p (s d)"), ident_b[:])
                    ins.then_inc(rec_turned.sem, 1)

                def unit(g, n, first=False):
                    M = (r * KV + g) * NU + n
                    qt, heads = UNITS[n]
                    keys = (qt + 1) * P
                    pair = unit_pair(first, n)
                    same = n > 0 and unit_pair(first, n - 1) == pair or first and n == 0
                    pe.wait_ge(unit_used.sem, unit_used.after(M - 1 if same else M - 2))
                    banks = psM[:, 2 * pair:2 * pair + 2, :].rearrange("p a b -> p (a b)")
                    for n_h, h in enumerate(heads):
                        at = n_h * keys if keys != 384 else n_h * 512
                        for k0 in range(0, keys, 512):
                            k1 = min(keys, k0 + 512)
                            diag = k1 == keys
                            ins = pe.matmul(banks[:, at + k0:at + k1], qT[0:MAXROW, g * REP + h, qt * P:(qt + 1) * P],
                                            kT[0:MAXROW, g, k0:k1], start=True, stop=not diag)
                        ins = pe.matmul(banks[:, at + keys - P:at + keys], ident_b[:], tri_b[:], start=False, stop=True)
                    ins.then_inc(unit_ready.sem, 1)

                def nm_turn(g, c, nm_ps):
                    n = (r * KV + g) * CHUNKS + c
                    pe.wait_ge(nm_split.sem, nm_split.after(n))
                    for qt in range(QT_PER_CHUNK):
                        ins = pe.transpose(nm_ps[0:3 * REP, qt * P:(qt + 1) * P],
                                           nm_parts[:, c, qt].rearrange("p a h -> p (a h)"), ident_b[:])
                    ins.then_inc(nm_turned.sem, 1)

                def scores(g, s, i):
                    c, kb, q0, w = STEPS[s]
                    if s in (0, FIRST_1) and i == 0:
                        pe.wait_ge(nm_in[c], (r * KV + g) * 16 + 32)
                    n = EXPS_BEFORE[s] + i
                    pe.wait_ge(p_ready.sem, p_ready.after((r * KV + g) * NE + n - 2))
                    for at, j in enumerate(head_batches(STEPS[s])[i]):
                        ins = pe.matmul(psE[:, n % 2, at * w:(at + 1) * w], kT[0:DEPTH, g, kb * P:(kb + 1) * P],
                                        qT[0:DEPTH, g * REP + j, q0:q0 + w], start=True, stop=True)
                    ins.then_inc(st_ready.sem, 1)

                def pv(g, s):
                    c, kb, q0, w = STEPS[s]
                    u = r * KV + g
                    off = q0 - c * QCHUNK
                    if s == 0:
                        pe.wait_ge(v_ready.sem, v_ready.after(u))
                    if kb == 0:
                        pe.wait_ge(o_copied.sem, o_copied.after(u * CHUNKS + (c - 1)))
                    if kb >= c * QT_PER_CHUNK:
                        pe.wait_ge(masked.sem, masked.after(u * ND + kb))
                    else:
                        pe.wait_ge(p_ready.sem, p_ready.after(u * NE + last_exp(s)))
                    for j in range(REP):
                        ins = pe.matmul(psO[VW * j:VW * (j + 1), off:off + w], v_grp[:, kb, :],
                                        probs[:, s % PSLOTS, j, 0:w], start=(kb == 0),
                                        stop=(kb == (c + 1) * QT_PER_CHUNK - 1), tile_position=(0, VW * j))
                    ins.then_inc(pv_done.sem, 1)

                def o_turn(g, c):
                    n = (r * KV + g) * CHUNKS + c
                    pe.wait_ge(o_copied.sem, o_copied.after(n))
                    turn(o_T[:, c, :], psT[:], o_turned)

                def turn_c(t, k):
                    if t == 0:
                        pe.wait_ge(unit_used.sem, unit_used.after(r * (KV * NU) + (KV * NU - 1)))
                    if t in (0, AHEAD):
                        pe.wait_ge(o_done.sem, o_done.after(r * (KV * CHUNKS) + (KV - 1) * CHUNKS + t // AHEAD))
                    wait_lo(c_turn(t) - 2)
                    turn(attn[:, t, :], psM[:, k, :], turned)

                def turn_d(t, k):
                    pe.wait_ge(xn_ready.sem, xn_ready.after(r * (2 * TILES) + (TILES + t)))
                    wait_lo(d_turn(t) - 2)
                    turn(xn[:, k, :], psM[:, k, :], turned)

                def project(X, k, his, los):
                    wait_hi(X)
                    if X - 2 >= TILES:
                        what, t = CD_TILES[X - 2 - TILES]
                        added = wo_added if what == "C" else ffn_added
                        pe.wait_ge(added.sem, added.after(r * TILES + t))
                    dst = psM[:, 2 + k, :]
                    some = products(his, los, 0, DIM)
                    multiply(k, dst, some[:-KC], True, False)
                    wait_lo(X)
                    multiply(k, dst, some[-KC:], False, True).then_inc(projected.sem, 1)

                def project_c(t, k):
                    if t == 0:
                        pe.wait_ge(wo_lo_done, r * KC + KC)
                    project(c_turn(t), k, wo_hi, w_lo)

                def project_d(t, k):
                    project(d_turn(t), k, wf_s, None)

                tiles = {"CT": turn_c, "CP": project_c, "DT": turn_d, "T": turn_d, "DP": project_d}

                def group(g, has_prev, has_next):
                    u = r * KV + g
                    for what, *arg in group_order(has_prev, has_next):
                        if what == "S":
                            scores(g, *arg)
                        elif what in tiles:
                            tiles[what](arg[0], arg[0] % 2)
                        elif what == "U":
                            unit(g + 1, arg[0])
                        elif what == "PV":
                            pv(g, arg[0])
                        elif what == "N":
                            c, d = arg
                            outs = u * CHUNKS - 1 if c == 1 else u * CHUNKS
                            if c == 1 and not has_prev:
                                outs = u * CHUNKS
                            pe.wait_ge(o_done.sem, o_done.after(outs - 1))
                            if not (c == 0 and d == 0):
                                pe.wait_ge(nm_copied.sem, nm_copied.after((u + d) * CHUNKS + (c - 1)))
                            nm_turn(g + d, c, nm_ps)
                        elif what == "O":
                            c, d = arg
                            pe.wait_ge(nm_copied.sem, nm_copied.after(
                                (u + 1) * CHUNKS if (c == 0 and has_next) else u * CHUNKS + 1))
                            pe.wait_ge(o_done.sem, o_done.after((u + d) * CHUNKS + (c - 1)))
                            o_turn(g + d, c)

                for n in SLOTS_A:
                    if n == SLOT_NM:
                        nm_turn(0, 0, nm_ps_0)
                    for what, arg, t in slot_work(PE_SLOT, n):
                        if what == "TX" and t > 0:
                            turn_xn(r, t, t % 2)
                        elif what == "Q":
                            qkv(t, t % 2, arg[0])
                        elif what == "R":
                            turn_rec(t, arg[0])
                        elif what == "U":
                            if arg[0] == 0:
                                pe.wait_ge(rec_dve.sem, rec_dve.after(r * (2 * TILES) + (t * 2 + 1)))
                                pe.wait_ge(rec_act.sem, rec_act.after(r * (3 * TILES) + (t * 3 + 2)))
                            unit(0, units_of(t)[arg[0]], first=True)

                pe.wait_ge(rec_act.sem, rec_act.after(r * (3 * TILES) + (3 * TILES - 1)))
                pe.wait_ge(rec_dve.sem, rec_dve.after(r * (2 * TILES) + (2 * TILES - 1)))
                group(0, False, True)
                with pe.Fori(1, KV - 1) as g:
                    group(g, True, True)
                group(KV - 1, True, False)
                for what, *arg in words(TAIL_ORDER):
                    if what in tiles:
                        tiles[what](arg[0], arg[0] % 2)
                    elif what == "O":
                        pe.wait_ge(o_done.sem, o_done.after(r * (KV * CHUNKS) + (KV - 1) * CHUNKS))
                        o_turn(KV - 1, 1)
                    elif what == "TA":
                        turn_xn(r + 1, 0, 0)

            pe.wait_ge(eye_in, 16)
            turn_xn(0, 0, 0)
            rounds(pe, round_)

        @block.scalar
        def _(act):
            act.preload_act_table_set("natural_log_exp_and_others")
            act.wait_ge(ready, 1)
            for s in (hi_ready, qkv_used, rec_act, p_ready, o_copied):
                act.sem_inc(s.sem, s.credit)

            def first_rstd(q, i):
                act.wait_ge(var_ready.sem, var_ready.after(q))
                act.activation(ln_var[:, i % 2], mv[:, i % 2, :, 1], ACT.Ln, bias=eps_s[:, 0:1]).then_inc(ln_done.sem, 1)
                act.wait_ge(ln_done.sem, ln_done.after(q))
                act.activation(rs0[:, i % 2], ln_var[:, i % 2], ACT.Exp, scale=-0.5).then_inc(rs_ready.sem, 1)

            def wq_split(n, c):
                if c == 0:
                    act.wait_ge(wq_in, n * 16 + 16)
                act.activation(wq_hi[:, c, :], wq_raw[:, c, :], ACT.Copy).then_inc(wq_hi_done, 1)

            def hi(r, X, src):
                act.wait_ge(turned.sem, turned.after(r * TURNS + X))
                act.wait_ge(projected.sem, projected.after(r * TURNS + (X - 2)))
                act.activation(xT_hi[:, X % 2].rearrange("p a b -> p (a b)"), src, ACT.Copy).then_inc(hi_ready.sem, 1)

            def round_(b, l, r):

                def rec_copy(t, q):
                    act.wait_ge(rec_turned.sem, rec_turned.after((r * TILES + t) * 5 + q))
                    act.activation(qT[:, 8 * q:8 * q + 8, t * P:(t + 1) * P],
                                   rec_banks[(t + q) % 2].rearrange("p (h n) -> p h n", h=8),
                                   ACT.Copy).then_inc(rec_act.sem, 1)

                def qkv_copy(t, k):
                    act.wait_ge(projected.sem, projected.after(r * TURNS + t))
                    bank = qkv_bank(t)
                    act.activation(qk[:, k, 0:DIM], psM[:, bank, :], ACT.Copy)
                    act.activation(qk[:, k, DIM:QK], psM[:, bank + 1, 0:QK - DIM], ACT.Copy).then_inc(qk_ready.sem, 1)
                    act.activation(vs[:, t], psM[:, bank + 1, QK - DIM:QKV - DIM].rearrange("p (h d) -> p h d", d=HD),
                                   ACT.Copy).then_inc(qkv_used.sem, 1)

                def part_h(t, k):
                    T = r * TILES + t
                    rq = r_s[:, k, 0:DIM].rearrange("p (h a d) -> p h a d", h=HEADS, a=1)
                    rk = r_s[:, k, DIM:QK].rearrange("p (h a d) -> p h a d", h=KV, a=1)
                    act.wait_ge(rec_turned.sem, rec_turned.after((T - RECS) * 5 + 4))
                    act.wait_ge(rope_ready.sem, rope_ready.after(T))
                    act.activation(q_rec[:, t % RECS, :, 0:3, :], rq.to_broadcast([P, HEADS, 3, HD]), ACT.Copy)
                    act.activation(k_rec[:, t % RECS, :, 1:6:2, :], rk.to_broadcast([P, KV, 3, HD]), ACT.Copy).then_inc(h_ready.sem, 1)

                def part_m(t, k):
                    tq = t_s[:, k, 0:DIM].rearrange("p (h a d) -> p h a d", h=HEADS, a=1)
                    tk = t_s[:, k, DIM:QK].rearrange("p (h a d) -> p h a d", h=KV, a=1)
                    act.wait_ge(r1_ready.sem, r1_ready.after(r * TILES + t))
                    act.activation(q_rec[:, t % RECS, :, 3:5, :], tq.to_broadcast([P, HEADS, 2, HD]), ACT.Copy)
                    act.activation(k_rec[:, t % RECS, :, 2:7:2, :], tk.to_broadcast([P, KV, 3, HD]), ACT.Copy).then_inc(m_ready.sem, 1)

                for n in SLOTS_A:
                    for what, arg, t in slot_work(ACT_SLOT, n):
                        if what == "HI" and t > 0:
                            hi(r, t, psE[:, t % 2, :])
                        elif what == "RC":
                            rec_copy(t, arg[0])
                        elif what == "PM":
                            part_m(t, t % 2)
                        elif what == "PH":
                            part_h(t, t % 2)
                        elif what == "QC":
                            qkv_copy(t, t % 2)
                        elif what == "RS":
                            first_rstd(r * (2 * PAIRS) + t, t)

                def exp(g, s, i):
                    w = STEPS[s][3]
                    if i == 0:
                        act.wait_ge(pv_done.sem, pv_done.after((r * KV + g) * NS + s - PSLOTS))
                    heads = head_batches(STEPS[s])[i]
                    n = EXPS_BEFORE[s] + i
                    act.wait_ge(st_ready.sem, st_ready.after((r * KV + g) * NE + n))
                    act.activation(probs[:, s % PSLOTS, heads[0]:heads[0] + len(heads), 0:w],
                                   psE[:, n % 2, 0:w * len(heads)].rearrange("p (h q) -> p h q", q=w),
                                   ACT.Exp).then_inc(p_ready.sem, 1)

                def o_copy(g, c):
                    n = (r * KV + g) * CHUNKS + c
                    last_step = FIRST_1 - 1 if c == 0 else NS - 1
                    act.wait_ge(pv_done.sem, pv_done.after((r * KV + g) * NS + last_step))
                    act.wait_ge(o_turned.sem, o_turned.after(n - CHUNKS))
                    act.activation(o_T[:, c, :], psO[:], ACT.Copy).then_inc(o_copied.sem, 1)

                def wo_split(c):
                    if c == 0:
                        act.wait_ge(wo_in, r * 16 + 16)
                    act.activation(wo_hi[:, c, :], wo_raw[:, c, :], ACT.Copy).then_inc(wo_hi_done, 1)

                def group(g, first=False):
                    for s in range(NS):
                        for i in range(len(head_batches(STEPS[s]))):
                            exp(g, s, i)
                        if first and s in WO_HI_AFTER:
                            wo_split(WO_HI_AFTER.index(s))
                        if s == FIRST_1 + 1:
                            o_copy(g, 0)
                    o_copy(g, 1)

                def other(what, n):
                    if what == "CT":
                        hi(r, c_turn(n), psM[:, n % 2, :])
                    elif what in ("DT", "H"):
                        hi(r, d_turn(n), psM[:, n % 2, :])
                    elif what == "LR":
                        first_rstd(r * (2 * PAIRS) + PAIRS + n, n)
                    elif what == "TA":
                        hi(r, TURNS, psE[:, 0, :])
                    elif what == "WQ":
                        wq_split(r + 1, n)

                group(0, first=True)
                with act.Fori(1, KV - 1) as g:
                    group(g)
                for what, *arg in words(LAST_ORDER):
                    if what == "S":
                        exp(KV - 1, *arg)
                    if (what, *arg) == ("S", FIRST_1, len(head_batches(STEPS[FIRST_1])) - 1):
                        o_copy(KV - 1, 0)
                    other(what, arg[0])
                o_copy(KV - 1, 1)
                for what, *arg in words(TAIL_ORDER):
                    other(what, arg[0])

            first_rstd(0, 0)
            hi(0, 0, psE[:, 0, :])
            for c in range(KC):
                wq_split(0, c)
            rounds(act, round_)

        @block.vector
        def _(dve):
            for s in (xn_ready, lo_ready, rec_ready, rec_dve, unit_used, o_done, wo_added, ffn_added):
                dve.sem_inc(s.sem, s.credit)
            dve.memset(v_grp[:, :, HD:HD + 1], 1.0)
            dve.memset(v_grp[:, :, HD + 1:VW], 0.0)
            dve.memset(eps_s[:], EPS).then_inc(ready, 1)

            def link(self, n, ins):
                ins.then_inc(self.sem, 1)
                wait_alone(dve, self.sem, self.after(n))

            def tile_of(i, k):
                if isinstance(i, int):
                    return xs[:, i * 2 + k, :]
                return xs[:, bass.ds(i * 2 + k, 1), :].rearrange("p a d -> p (a d)")

            def ln_stats(q, i):
                for k in range(2):
                    ins = dve.bn_stats(stats[:, i % 2, k, :], tile_of(i % PAIRS, k))
                link(ls_self, q * LS_LINKS, ins)
                dve.bn_aggr(mv[:, i % 2, 0, :], stats[:, i % 2, 0, :])
                dve.bn_aggr(mv[:, i % 2, 1, :], stats[:, i % 2, 1, :]).then_inc(var_ready.sem, 1)
                wait_alone(dve, var_ready.sem, var_ready.after(q))
                link(ls_self, q * LS_LINKS + 1, dve.tensor_scalar(var_eps[:, i % 2], mv[:, i % 2, :, 1], EPS, None, ALU.add))

            def ln_newton(q, i):
                dve.wait_ge(rs_ready.sem, rs_ready.after(q))
                y = rs0[:, i % 2]
                link(lm_self, q * LM_LINKS, dve.tensor_tensor(newton[:], y, y, ALU.mult))
                link(lm_self, q * LM_LINKS + 1, dve.tensor_tensor(newton2[:], newton[:], var_eps[:, i % 2], ALU.mult))
                link(lm_self, q * LM_LINKS + 2, dve.tensor_scalar(newton[:], newton2[:], -0.5, 1.5, ALU.mult, ALU.add))
                dve.tensor_tensor(rstd[:, i % 2], y, newton[:], ALU.mult).then_inc(lm_self.sem, 1)

            def ln_apply(q, i):
                wait_alone(dve, lm_self.sem, lm_self.after(q * LM_LINKS + 3))
                for k in range(2):
                    dve.tensor_scalar(xn[:, k, :], tile_of(i % PAIRS, k), mv[:, i % 2, k, 0:1], rstd[:, i % 2, k:k + 1],
                                      ALU.subtract, ALU.mult).then_inc(xn_ready.sem, 1)

            def ln_a_stats(r, b, i):
                dve.wait_ge(x_in[i], b * 16 + 16)
                wait_alone(dve, ffn_added.sem, ffn_added.after(r * TILES - TILES + i * 2 + 1))
                ln_stats(r * (2 * PAIRS) + i, i)

            def ln_a(r, i):
                ln_newton(r * (2 * PAIRS) + i, i)
                wait_alone(dve, turned.sem, turned.after(r * TURNS + i * 2 - 1))
                ln_apply(r * (2 * PAIRS) + i, i)

            def lo(r, X, src):
                dve.wait_ge(hi_ready.sem, hi_ready.after(r * TURNS + X))
                k = X % 2
                dve.tensor_tensor(xT_lo[:, k].rearrange("p a b -> p (a b)"), src,
                                  xT_hi[:, k].rearrange("p a b -> p (a b)").bitcast(F32), ALU.subtract).then_inc(lo_ready.sem, 1)

            ln_a_stats(0, 0, 0)
            ln_a(0, 0)
            lo(0, 0, psE[:, 0, :])
            for c in range(1, KC):
                dve.wait_ge(wq_hi_done, c + 1)
                dve.tensor_tensor(w_lo[:, c, :], wq_raw[:, c, :], wq_hi[:, c, :].bitcast(F32), ALU.subtract).then_inc(wq_lo_done, 1)
            dve.wait_ge(consts_in, 16 * 5)
            dve.tensor_copy(ident_b[:], ident[:])
            dve.tensor_copy(tri_b[:], rows[:, 0:P]).then_inc(ready, 1)

            def round_(b, l, r):

                def rec_copy(t, q):
                    dve.wait_ge(rec_turned.sem, rec_turned.after((r * TILES + t) * 5 + q))
                    to = qT[:, 8 * q:8 * q + 8, t * P:(t + 1) * P] if q < 4 else kT[:, :, t * P:(t + 1) * P]
                    dve.tensor_copy(to, rec_banks[(t + q) % 2].rearrange("p (h n) -> p h n", h=8)).then_inc(rec_dve.sem, 1)

                def rope_cos(t, k):
                    T = r * TILES + t
                    dve.wait_ge(qk_ready.sem, qk_ready.after(T))
                    c = cos_s[:, bass.ds(l, 1), t, :]
                    dve.tensor_tensor(r_s[:, k].rearrange("p (h d) -> p h d", d=HD),
                                      qk[:, k].rearrange("p (h d) -> p h d", d=HD),
                                      c.to_broadcast([P, HEADS + KV, HD]), ALU.mult).then_inc(cos_self.sem, 1)

                def rope(t, k):
                    T = r * TILES + t
                    dve.wait_ge(cos_self.sem, cos_self.after(T))
                    dve.wait_ge(sin_ready.sem, sin_ready.after(T))
                    dve.tensor_tensor(r_s[:, k], r_s[:, k], t_s[:, k], ALU.add).then_inc(rope_ready.sem, 1)

                def part_l(t, k):
                    dve.wait_ge(m_ready.sem, m_ready.after(r * TILES + t))
                    tq = t_s[:, k, 0:DIM].rearrange("p (h a d) -> p h a d", h=HEADS, a=1)
                    tk = t_s[:, k, DIM:QK].rearrange("p (h d) -> p h d", h=KV)
                    dve.tensor_tensor(q_rec[:, t % RECS, :, 5:7, :], tq.to_broadcast([P, HEADS, 2, HD]),
                                      q_rec[:, t % RECS, :, 3:5, :], ALU.subtract)
                    dve.tensor_tensor(k_rec[:, t % RECS, :, 0, :], tk, k_rec[:, t % RECS, :, 2, :], ALU.subtract).then_inc(rec_ready.sem, 1)

                def unit(g, n, first=False):
                    M = (r * KV + g) * NU + n
                    qt, heads = UNITS[n]
                    keys = (qt + 1) * P
                    if n in (0, UNITS_0):
                        dve.wait_ge(nm_split.sem, nm_split.after((r * KV + g - 1) * CHUNKS + (0 if n == 0 else 1)))
                    dve.wait_ge(unit_ready.sem, unit_ready.after(M))
                    pair = unit_pair(first, n)
                    banks = psM[:, 2 * pair:2 * pair + 2, :].rearrange("p a b -> p (a b)")
                    pitch = keys if keys != 384 else 512
                    src = banks[:, 0:pitch * len(heads)].rearrange("p (h k) -> p h k", k=pitch)[:, :, 0:keys]
                    dve.tensor_reduce(mx[:, qt, heads[0]:heads[0] + len(heads)], src, AX.X, ALU.max).then_inc(unit_used.sem, 1)

                def nm_copy(g, c, nm_ps=nm_ps):
                    u = r * KV + g
                    dve.wait_ge(nm_turned.sem, nm_turned.after(u * CHUNKS + c))
                    dve.wait_ge(nm_in[c], u * 16 + 16)
                    dve.tensor_copy(nm_rows[:, c, :], nm_ps[0:3 * REP, 0:QCHUNK]).then_inc(nm_copied.sem, 1)

                def o_divide(g, c):
                    n = (r * KV + g) * CHUNKS + c
                    dve.wait_ge(o_turned.sem, o_turned.after(n))
                    o = psT[:].rearrange("p (t h d) -> p t h d", t=QT_PER_CHUNK, h=REP)
                    dve.reciprocal(den[:], o[:, :, :, HD]).then_inc(o_self.sem, 1)
                    dve.wait_ge(o_self.sem, o_self.after(n))
                    to = attn[:, c * QT_PER_CHUNK:(c + 1) * QT_PER_CHUNK, bass.ds(g * (REP * HD), REP * HD)]
                    dve.tensor_tensor(to.rearrange("p t (h d) -> p t h d", h=REP), o[:, :, :, 0:HD],
                                      den[:].rearrange("p t (h a) -> p t h a", a=1).to_broadcast([P, QT_PER_CHUNK, REP, HD]),
                                      ALU.mult).then_inc(o_done.sem, 1)

                def group(g, has_prev, has_next):
                    for what, *arg in group_order(has_prev, has_next):
                        if what == "U":
                            unit(g + 1, arg[0])
                        elif what == "N":
                            nm_copy(g + arg[1], arg[0])
                        elif what == "O":
                            o_divide(g + arg[1], arg[0])

                for n in SLOTS_A:
                    if n == SLOT_NM:
                        nm_copy(0, 0, nm_ps_0)
                    for what, arg, t in slot_work(DVE_SLOT, n):
                        if what == "LO" and t > 0:
                            lo(r, t, psE[:, t % 2, :])
                        elif what == "RC":
                            rec_copy(t, arg[0])
                        elif what == "U":
                            unit(0, units_of(t)[arg[0]], first=True)
                        elif what == "COS":
                            rope_cos(t, t % 2)
                        elif what == "ROPE":
                            rope(t, t % 2)
                        elif what == "PL":
                            part_l(t, t % 2)
                        elif what == "ST":
                            ln_a_stats(r, b, t)
                        elif what == "AP":
                            ln_a(r, t)

                group(0, False, True)
                wait_alone(dve, wo_lo_done, r * KC + KC)
                with dve.Fori(1, KV - 1) as g:
                    group(g, True, True)

                def add_wo(t):
                    dve.wait_ge(projected.sem, projected.after(r * TURNS + c_turn(t)))
                    dve.tensor_tensor(xs[:, t, :], psM[:, 2 + t % 2, :], xs[:, t, :], ALU.add).then_inc(wo_added.sem, 1)

                def add_ffn(t):
                    dve.wait_ge(projected.sem, projected.after(r * TURNS + d_turn(t)))
                    dve.scalar_tensor_tensor(out=xs[:, t, :], in0=psM[:, 2 + t % 2, :], scalar=scale_s[:, 0:1],
                                             in1=xs[:, t, :], op0=ALU.mult, op1=ALU.add).then_inc(ffn_added.sem, 1)

                def ln_d_stats(i):
                    if i < PAIRS:
                        wait_alone(dve, wo_added.sem, wo_added.after(r * TILES + i * 2 + 1))
                    else:
                        dve.wait_ge(x_in[0], (b + l) * 16 + 16)
                        wait_alone(dve, ffn_added.sem, ffn_added.after(r * TILES + 1))
                    ln_stats(r * (2 * PAIRS) + PAIRS + i, i)

                def ln_d(i):
                    last = TILES - 1 if i == 0 else d_turn(2 * i - 1)
                    wait_alone(dve, turned.sem, turned.after(r * TURNS + last))
                    ln_apply(r * (2 * PAIRS) + PAIRS + i, i)

                def other(what, n):
                    if what == "CT":
                        lo(r, c_turn(n), psM[:, n % 2, :])
                    elif what in ("DT", "H"):
                        lo(r, d_turn(n), psM[:, n % 2, :])
                    elif what == "CP":
                        add_wo(n)
                    elif what == "DP":
                        add_ffn(n)
                    elif what == "LS":
                        ln_d_stats(n)
                    elif what == "LN":
                        ln_d(n)
                    elif what == "LM":
                        ln_newton(r * (2 * PAIRS) + PAIRS + n, n)
                    elif what == "TA":
                        lo(r, TURNS, psE[:, 0, :])

                for what, *arg in words(LAST_ORDER):
                    if what == "N":
                        nm_copy(KV - 1, 1)
                    elif what == "O":
                        o_divide(KV - 1 + arg[1], arg[0])
                    else:
                        other(what, arg[0])
                for what, *arg in words(TAIL_ORDER):
                    if what == "O":
                        o_divide(KV - 1, 1)
                    else:
                        other(what, arg[0])

            rounds(dve, round_)

        @block.gpsimd
        def _(pool):
            pool.sem_inc(nm_split.sem, nm_split.credit)

            def wq_split(n, chunks=range(KC)):
                for c in chunks:
                    wait_alone(pool, wq_hi_done, n * KC + (c + 1))
                    pool.tensor_tensor(w_lo[:, c, :], wq_raw[:, c, :], wq_hi[:, c, :].bitcast(F32),
                                       ALU.subtract).then_inc(wq_lo_done, 1)

            def round_(b, l, r):
                def rope_sin(t, k):
                    T = r * TILES + t
                    wait_alone(pool, qk_ready.sem, qk_ready.after(T))
                    wait_alone(pool, rec_ready.sem, rec_ready.after(T - 2))
                    x4 = qk[:, k].rearrange("p (h a d) -> p h a d", a=2, d=HALF)
                    t4 = t_s[:, k].rearrange("p (h a d) -> p h a d", a=2, d=HALF)
                    sn = sin_s[:, bass.ds(l, 1), t, :]
                    for a in range(2):
                        ins = pool.tensor_tensor(t4[:, :, a, :], x4[:, :, 1 - a, :],
                                                 sn[:, :, a * HALF:(a + 1) * HALF].to_broadcast([P, HEADS + KV, HALF]), ALU.mult)
                    ins.then_inc(sin_ready.sem, 1)

                def rest(t, k):
                    wait_alone(pool, h_ready.sem, h_ready.after(r * TILES + t))
                    rq = r_s[:, k, 0:DIM].rearrange("p (h d) -> p h d", d=HD)
                    rk = r_s[:, k, DIM:QK].rearrange("p (h d) -> p h d", d=HD)
                    tq = t_s[:, k, 0:DIM].rearrange("p (h d) -> p h d", d=HD)
                    tk = t_s[:, k, DIM:QK].rearrange("p (h d) -> p h d", d=HD)
                    pool.tensor_tensor(tq, rq, q_rec[:, t % RECS, :, 0, :], ALU.subtract)
                    pool.tensor_tensor(tk, rk, k_rec[:, t % RECS, :, 1, :], ALU.subtract).then_inc(r1_ready.sem, 1)

                wait_alone(pool, wq_lo_done, r * KC + KC)
                pool.memset(q_rec_last, 0.0)
                pool.memset(k_rec[:, :, :, SLOTS - 1, 3:HD], 0.0)
                pool.memset(k_rec[:, :, :, SLOTS - 1, 0:3], 1.0)
                for n in range(1, TILES + 2):
                    if 0 <= n - 2 < TILES:
                        rest(n - 2, n % 2)
                    if n - 1 < TILES:
                        rope_sin(n - 1, (n - 1) % 2)

                def nm_parts_of(g, c):
                    n = (r * KV + g) * CHUNKS + c
                    links = [0]

                    def link(ins):
                        ins.then_inc(nm_self.sem, 1)
                        wait_alone(pool, nm_self.sem, nm_self.after(n * NM_LINKS + links[0]))
                        links[0] += 1

                    last_unit = UNITS_0 - 1 if c == 0 else NU - 1
                    wait_alone(pool, unit_used.sem, unit_used.after((r * KV + g) * NU + last_unit))
                    wait_alone(pool, nm_turned.sem, nm_turned.after(n - 2))
                    link(pool.tensor_scalar(nm[:], mx[:, c * QT_PER_CHUNK:(c + 1) * QT_PER_CHUNK, :], -1.0, None, ALU.mult))
                    link(pool.tensor_copy(nm_parts[:, c, :, 0, :], nm[:]))
                    link(pool.tensor_tensor(nm_r[:], nm[:], nm_parts[:, c, :, 0, :], ALU.subtract))
                    link(pool.tensor_copy(nm_parts[:, c, :, 1, :], nm_r[:]))
                    pool.tensor_tensor(nm_parts[:, c, :, 2, :], nm_r[:], nm_parts[:, c, :, 1, :], ALU.subtract).then_inc(nm_split.sem, 1)
                    assert links[0] == NM_LINKS

                def mask(g, s):
                    u = r * KV + g
                    wait_alone(pool, p_ready.sem, p_ready.after(u * NE + last_exp(s)))
                    d = probs[:, s % PSLOTS, :, 0:P]
                    pool.affine_select(out=d, in_=d, compare_op=ALU.is_ge, fill=0.0, base=0,
                                       pattern=[[0, REP], [1, P]], channel_multiplier=-1).then_inc(masked.sem, 1)

                def wo_split(c):
                    wait_alone(pool, wo_hi_done, r * KC + (c + 1))
                    pool.tensor_tensor(w_lo[:, c, 0:DIM], wo_raw[:, c, :], wo_hi[:, c, :].bitcast(F32),
                                       ALU.subtract).then_inc(wo_lo_done, 1)

                def group(g, has_next, first=False):
                    u = r * KV + g
                    wait_alone(pool, pv_done.sem, pv_done.after(u * NS - 1))
                    pool.tensor_copy(v_grp[:, :, 0:HD], vs[:, :, bass.ds(g, 1), :].rearrange("p t a d -> p t (a d)")).then_inc(v_ready.sem, 1)
                    for s in DIAGONAL:
                        mask(g, s)
                        if has_next and s == SPLIT_AFTER:
                            nm_parts_of(g + 1, 0)
                        if first and s in WO_LO_AFTER:
                            wo_split(WO_LO_AFTER.index(s))
                    if has_next:
                        nm_parts_of(g + 1, 1)

                nm_parts_of(0, 0)
                nm_parts_of(0, 1)
                group(0, True, first=True)
                with pool.Fori(1, KV - 1) as g:
                    group(g, True)
                group(KV - 1, False)
                wait_alone(pool, projected.sem, projected.after(r * TURNS + c_turn(TILES - 1)))
                wq_split(r + 1)

            wq_split(0, range(0, 1))
            pool.wait_ge(consts_in, 16 * 5)
            pool.tensor_scalar(wf_s[:], wf_raw, 2.0, -1.0, ALU.mult, ALU.add).then_inc(ready, 1)
            pool.wait_ge(ready, READY)
            rounds(pool, round_)


def tables():
    import numpy as np
    cos, sin = [], []
    for base in (10000.0, 500000.0):
        inv = (np.float32(1.0) / np.power(np.float32(base), np.arange(0, HD, 2, dtype=np.float32) / np.float32(HD))).astype(np.float32)
        ang = (np.arange(SEQ, dtype=np.float32)[:, None] * inv[None, :]).astype(np.float64)
        c, s = 0.5 * np.cos(ang), 0.5 * np.sin(ang)
        cos.append(np.concatenate([c, c], 1))
        sin.append(np.concatenate([-s, s], 1))
    shape = lambda a: np.ascontiguousarray(np.stack(a).astype(np.float32).reshape(LAYERS, TILES, P, HD).transpose(2, 0, 1, 3))
    return shape(cos), shape(sin)


def kernel(L0_attn_a_x, L0_attn_a_w_qkv, L0_attn_a_w_o, L0_attn_b_w_qkv, L0_attn_b_w_o, L0_ffn_kernel, L0_ffn_scale):
    import numpy as np
    import concourse.bacc as bacc
    from concourse.bass_utils import run_bass_kernel_spmd

    wa = np.asarray(L0_attn_a_w_qkv)
    wa_qk = wa[:, :QK].reshape(DIM, QK // HD, HALF, 2).transpose(0, 1, 3, 2).reshape(DIM, QK)
    wa = np.concatenate([wa_qk, wa[:, QK:]], 1)
    wb = np.asarray(L0_attn_b_w_qkv).T
    cos, sin = tables()
    tri = np.where(np.arange(P)[None, :] > np.arange(P)[:, None], np.float32(-1e30), np.float32(0)).astype(np.float32)
    arrays = {
        "x": np.ascontiguousarray(L0_attn_a_x),
        "w_qkv": np.ascontiguousarray(np.stack([wa, wb])),
        "w_o": np.ascontiguousarray(np.stack([np.asarray(L0_attn_a_w_o), np.asarray(L0_attn_b_w_o).T])),
        "w_ffn": np.ascontiguousarray(L0_ffn_kernel),
        "scale": np.ascontiguousarray(np.asarray(L0_ffn_scale).reshape(1)),
        "cos": cos,
        "sin": sin,
        "eye": np.eye(P, dtype=np.float32),
        "tri": tri,
    }
    nc = bacc.Bacc("TRN2", target_bir_lowering=False, num_devices=1)
    args = [nc.dram_tensor(f"in_{n}", a.shape, mybir.dt.from_np(a.dtype), kind="ExternalInput").ap() for n, a in arrays.items()]
    out = nc.dram_tensor("out_x", (BATCH, SEQ, DIM), F32, kind="ExternalOutput").ap()
    build(nc, *args, out)
    res = run_bass_kernel_spmd(nc, [{f"in_{n}": a for n, a in arrays.items()}], core_ids=[0])
    return res.results[0]["out_x"]
```
